# Optimizing a Trainium2 kernel written in Bass

```python
import numpy as np
import jax
import jax.numpy as jnp

def _softmax(x, axis=-1):
    return jax.nn.softmax(x, axis=axis)

def _gelu(x):
    return jax.nn.gelu(x, approximate=True)

def _silu(x):
    return jax.nn.silu(x)

def _sigmoid(x):
    return jax.nn.sigmoid(x)

def _layernorm(x, axis=-1, eps=1e-05):
    m = jnp.mean(x, axis=axis, keepdims=True)
    v = jnp.var(x, axis=axis, keepdims=True)
    return (x - m) / jnp.sqrt(v + eps)

def _scatter_add(tgt, idx, src, axis=0):
    return tgt.at[idx].add(src)

def _segment_sum(src, seg, n):
    return jax.ops.segment_sum(src, seg, n)
kernel_name = 'mk_adaln_d1_jaxref_r8_f36996'

def setup_inputs(seed: int=0):
    np.random.seed(seed)
    _w = jnp.asarray

    def _L0_attn_setup():
        import jax, jax.numpy as jnp
        import numpy as np
        NH = 16
        key = jax.random.key(seed)
        ks = jax.random.split(key, 5)
        B, T, D = (2, 256, 256)
        scale = 0.02
        return {'x': jax.random.normal(ks[0], (B, T, D), dtype=jnp.float32), 'Wq': jax.random.normal(ks[1], (D, D), dtype=jnp.float32) * scale, 'Wk': jax.random.normal(ks[2], (D, D), dtype=jnp.float32) * scale, 'Wv': jax.random.normal(ks[3], (D, D), dtype=jnp.float32) * scale, 'Wo': jax.random.normal(ks[4], (D, D), dtype=jnp.float32) * scale}
    _L0_attn_in = _L0_attn_setup()

    def _L0_ffn_setup():
        import jax, jax.numpy as jnp
        import numpy as np
        TOP_K = 2
        key = jax.random.key(seed)
        ks = jax.random.split(key, 5)
        B, S, D, F, E = (2, 128, 256, 512, 8)
        scale_in = 1.0 / np.sqrt(D)
        scale_f = 1.0 / np.sqrt(F)
        return {'hidden_states': jax.random.normal(ks[0], (B, S, D), dtype=jnp.float32), 'gate_w': jax.random.normal(ks[1], (D, E), dtype=jnp.float32) * scale_in, 'w1': jax.random.normal(ks[2], (E, D, F), dtype=jnp.float32) * scale_in, 'w3': jax.random.normal(ks[3], (E, D, F), dtype=jnp.float32) * scale_in, 'w2': jax.random.normal(ks[4], (E, F, D), dtype=jnp.float32) * scale_f}
    _L0_ffn_in = _L0_ffn_setup()
    _L0_c = _w((lambda *s: np.random.randn(*s).astype(np.float32) * 0.05)(4, 256))
    _L0_wmod = _w((lambda *s: np.random.randn(*s).astype(np.float32) * 0.05)(256, 6 * 256) * 256 ** (-0.5))
    _d = {'L0_attn_x': _L0_attn_in['x'], 'L0_attn_Wq': _L0_attn_in['Wq'], 'L0_attn_Wk': _L0_attn_in['Wk'], 'L0_attn_Wv': _L0_attn_in['Wv'], 'L0_attn_Wo': _L0_attn_in['Wo'], 'L0_ffn_gate_w': _L0_ffn_in['gate_w'], 'L0_ffn_w1': _L0_ffn_in['w1'], 'L0_ffn_w3': _L0_ffn_in['w3'], 'L0_ffn_w2': _L0_ffn_in['w2'], 'L0_c': _L0_c, 'L0_wmod': _L0_wmod}
    _x0 = _d['L0_attn_x']
    _d['L0_attn_x'] = jax.random.normal(jax.random.fold_in(jax.random.key(seed), 1), (4, 512, 256), dtype=_x0.dtype)
    del _x0
    return _d

def reference(L0_attn_x, L0_attn_Wq, L0_attn_Wk, L0_attn_Wv, L0_attn_Wo, L0_ffn_gate_w, L0_ffn_w1, L0_ffn_w3, L0_ffn_w2, L0_c, L0_wmod):

    def _L0_attn_ref(x, Wq, Wk, Wv, Wo):
        import jax, jax.numpy as jnp
        import numpy as np
        NH = 16
        B, T, D = x.shape
        hd = D // NH
        q = (x @ Wq.T).reshape(B, T, NH, hd).transpose(0, 2, 1, 3)
        k = (x @ Wk.T).reshape(B, T, NH, hd).transpose(0, 2, 1, 3)
        v = (x @ Wv.T).reshape(B, T, NH, hd).transpose(0, 2, 1, 3)
        att = jnp.einsum('bhtd,bhsd->bhts', q, k) / jnp.sqrt(jnp.asarray(hd, x.dtype))
        neg = jnp.finfo(att.dtype).min
        mask = jnp.triu(jnp.full((T, T), neg, dtype=att.dtype), k=1)
        att = att + mask
        w = jax.nn.softmax(att, axis=-1)
        z = jnp.einsum('bhts,bhsd->bhtd', w, v)
        z = z.transpose(0, 2, 1, 3).reshape(B, T, D)
        return z @ Wo.T

    def _L0_ffn_ref(hidden_states, gate_w, w1, w3, w2):
        import jax, jax.numpy as jnp
        import numpy as np
        TOP_K = 2
        orig_shape = hidden_states.shape
        D = orig_shape[-1]
        x = hidden_states.reshape(-1, D)
        E = gate_w.shape[-1]
        router_logits = (x @ gate_w).astype(jnp.float32)
        probs = jax.nn.softmax(router_logits, axis=-1)
        topk_vals, topk_idx = jax.lax.top_k(probs, TOP_K)
        onehot = jax.nn.one_hot(topk_idx, E, dtype=probs.dtype)
        combine = jnp.einsum('tke,tk->te', onehot, topk_vals)
        gate = jax.nn.silu(jnp.einsum('td,edf->etf', x, w1))
        up = jnp.einsum('td,edf->etf', x, w3)
        expert_out = jnp.einsum('etf,efd->etd', gate * up, w2)
        y = jnp.einsum('te,etd->td', combine, expert_out)
        return y.reshape(orig_shape)
    x = L0_attn_x
    mod = (_silu(L0_c) @ L0_wmod).reshape(L0_c.shape[0], 6, 1, -1)
    sa, ca, ga, sb, cb, gb = (mod[:, 0], mod[:, 1], mod[:, 2], mod[:, 3], mod[:, 4], mod[:, 5])
    ga = (2 * (ga >= 0) - 1) * jnp.maximum(jnp.abs(ga), 0.25)
    gb = (2 * (gb >= 0) - 1) * jnp.maximum(jnp.abs(gb), 0.25)
    h = _layernorm(x, axis=-1) * (1 + ca) + sa
    x = x + ga * _L0_attn_ref(h, L0_attn_Wq, L0_attn_Wk, L0_attn_Wv, L0_attn_Wo)
    h = _layernorm(x, axis=-1) * (1 + cb) + sb
    x = x + gb * _L0_ffn_ref(h, L0_ffn_gate_w, L0_ffn_w1, L0_ffn_w3, L0_ffn_w2)
    return x

_drawn_inputs = setup_inputs


def setup_inputs(seed=0):
    import zlib

    import numpy as np

    out = dict(_drawn_inputs(seed))
    spreads = {}
    factors = {'L0_attn_Wq': 8.0, 'L0_attn_Wk': 8.0, 'L0_attn_Wv': 8.0, 'L0_attn_Wo': 8.0}
    for name, (base, spread) in spreads.items():
        noise = np.random.default_rng([zlib.crc32(name.encode()), seed]).standard_normal(out[name].shape)
        drawn = base * np.exp(spread * noise) if base else spread * noise
        out[name] = jnp.asarray(drawn.astype(out[name].dtype))
    for name, factor in factors.items():
        out[name] = (out[name] * factor).astype(out[name].dtype)
    return out
```

```python
from contextlib import ExitStack

import concourse.bass as bass
from concourse import mybir

F32 = mybir.dt.float32
BF16 = mybir.dt.bfloat16
I32 = mybir.dt.int32
ALU = mybir.AluOpType
ACT = mybir.ActivationFunctionType
AX_X = mybir.AxisListType.X

P = 128
B, T, D = 4, 512, 256
NH, HD = 16, 16
E, F = 8, 512
N = B * T
DK = D // P
FK = F // P
TT = T // P
NT = N // P
EPS = 1e-5

HU = NH // 2
UNITS = B * 2
HG = 4
GROUPS = UNITS * HU // HG
NTERMS = 6
KS = NTERMS * HD
KB = KS + 3
Q_PART = (0, 0, 0, 1, 1, 2)
K_PART = (0, 1, 2, 0, 1, 0)
STACKS = 3

REGION = N + P
ROW = D + 2
DEST, WEIGHT = D, D + 1
NULL_ROW = E * REGION
HS_ROWS = E * REGION + P
TILES = 2 * N // P + E - 1
WCOLS = 2 * DK * F + FK * D
EARLY = 1
W1, W3, W2 = 0, DK * F, 2 * DK * F
NEG = -3.0e38


def merged(*streams):
    out = []
    for order, (steps, a, b) in enumerate(streams):
        out += [(a + (b - a) * (j + 0.5) / len(steps), order, j, s) for j, s in enumerate(steps)]
    return [s for *_, s in sorted(out, key=lambda x: x[:3])]


def attention_steps():
    rounds = []
    for s in range(-2, UNITS + 1):
        project, finish = [], []
        u = s + 2
        if u < UNITS:
            b = u // 2
            if u % 2 == 0:
                project += [("norm_stats", b), ("norm_rows", b), ("h_cols", b, 0), ("h_cols", b, 1)]
            project += [("project", u, 0), ("project", u, 1)]
            if u % 2 == 0:
                project += [("values", b, i) for i in range(TT)]
            project += [("split", u, 0), ("split", u, 1)]
        back = []
        if s >= 2:
            b, half = (s - 2) // 2, s % 2
            if s == UNITS:
                tiles = [b * TT + i for i in range(TT)]
            else:
                tiles = [b * TT + 2 * half, b * TT + 2 * half + 1]
            kinds = ("z_rows", "z_cols", "out_rows", "norm2", "h2_cols", "router")
            lag = 2
            for n in range(lag * (len(tiles) - 1) + len(kinds)):
                for j, t in enumerate(tiles):
                    if 0 <= n - lag * j < len(kinds):
                        back.append((kinds[n - lag * j], t))
            if half or s == UNITS:
                finish = [("gate", b), ("choose", b), ("rank", b), ("scatter", b)]
        streams = []
        if 0 <= s < UNITS:
            attend = []
            for g in (2 * s, 2 * s + 1):
                attend += [("score", g, n) for n in range(6)]
            for g, at in ((2 * s, 4), (2 * s + 1, 14)):
                for k, d in enumerate((0, 3, 5, 7)):
                    attend.insert(at + d, ("value_sum", g, k))
            streams.append((attend, 0.0, 1.0))
        if 0 <= s + 1 < UNITS:
            u = s + 1
            maxima = [("max_fill", u, n) for n in range(22)]
            streams += [(maxima, 0.0, 0.75), ([("max_rows", u)], 0.76, 0.78), ([("max_split", u)], 0.84, 0.86)]
        if project:
            streams.append((project, 0.02, 0.6))
        if back:
            streams.append((back, 0.05, 0.9))
        if finish:
            streams.append((finish, 0.9, 1.0))
        rounds += merged(*streams)
    return rounds


def max_fill(n):
    if n < 2:
        return 0, 4 * n, 4
    if n < 6:
        return 1, 2 * (n - 2), 2
    i = 2 + (n - 6) // HU
    return i, (n - 6) % HU, 1


def score_slot(n):
    return ((0, 0, 2), (0, 2, 2), (1, 0, 2), (1, 2, 2), (2, 0, 4), (3, 0, 4))[n]


def build(nc, x, wq, wk, wv, wo, gate_w, w1, w3, w2, c, wmod, out):
    with ExitStack() as ctx:
        def sb(name, shape, dt=F32):
            return ctx.enter_context(nc.sbuf_tensor(name, shape, dt))

        def sem(name):
            return ctx.enter_context(nc.semaphore(name))

        split_dram = nc.dram_tensor("split_dram", [UNITS, 2, P, 3, T], BF16)
        max_dram = nc.dram_tensor("max_dram", [UNITS, HU, 3, T], BF16)
        mod_dram = nc.dram_tensor("mod_dram", [B, 6 * D], F32)
        routed_dram = nc.dram_tensor("routed_dram", [HS_ROWS, ROW], F32)
        expert_dram = nc.dram_tensor("expert_dram", [2 * N + P, D], F32)

        arena = sb("arena", [P, EARLY * WCOLS + 28160 + TT * D + 4 * T])
        weights = arena[:, 0:E * WCOLS].rearrange("p (e n) -> p e n", e=E)
        place = [EARLY * WCOLS]

        def scratch(cols):
            place[0] += cols
            return arena[:, place[0] - cols:place[0]]

        q_stack = [scratch(HU * T // 2).bitcast(BF16).rearrange("p (h t) -> p h t", h=HU) for _ in range(STACKS)]
        k_stack = [scratch(HU * T // 2).bitcast(BF16).rearrange("p (h t) -> p h t", h=HU) for _ in range(STACKS)]
        probs_all = scratch(HG * (512 + 384 + 256 + 128))
        v_rows = [scratch(TT * NH * 32).rearrange("p (i h d) -> p i h d", i=TT, h=NH) for _ in range(2)]
        h_cols = [scratch(DK * T).rearrange("p (j t) -> p j t", j=DK) for _ in range(2)]
        z_cols = [scratch(4 * T).rearrange("p (g t) -> p g t", g=4) for _ in range(2)]
        parts = [scratch(3 * T // 2).bitcast(BF16).rearrange("p (a t) -> p a t", a=3) for _ in range(2)]
        rest = [scratch(T) for _ in range(2)]
        xn_all = scratch(TT * D)
        xn = xn_all.rearrange("p (i d) -> p i d", i=TT)
        tab_a = xn_all[0:1, 0:TILES * E].rearrange("p (k e) -> p k e", e=E)
        tab_b = xn_all[0:1, TILES * E:2 * TILES * E].rearrange("p (k e) -> p k e", e=E)
        probs, at = [], 0
        for k in range(TT):
            w = T - k * P
            probs.append(probs_all[:, at:at + HG * w].rearrange("p (h t) -> p h t", h=HG))
            at += HG * w
        wmod_sb = probs_all[:, 0:DK * 6 * D].rearrange("p (j n) -> p j n", j=DK)
        mod_rows = probs_all[0:B, DK * 6 * D:DK * 6 * D + 6 * D]
        place[0] = E * WCOLS
        xg = scratch(ROW)
        place[0] += ROW % 2
        xg_cols = scratch(D).rearrange("p (j t) -> p j t", j=DK)
        silu_sb = scratch(F)
        hidden = scratch(F)
        hidden_cols = scratch(F).rearrange("p (j t) -> p j t", j=FK)
        y_rows = scratch(D)
        tail = [scratch(2) for _ in range(2)]
        ya = arena[:, 0:NT * D].rearrange("p (t d) -> p t d", t=NT)
        yb = arena[:, NT * D:2 * NT * D].rearrange("p (t d) -> p t d", t=NT)

        xs = sb("xs", [P, NT, D])
        wqk_sb = sb("wqk_sb", [P, 2, DK, D])
        wv_sb = sb("wv_sb", [P, DK, D])
        wo_sb = sb("wo_sb", [P, DK, D])
        wog = sb("wog", [P, DK, D])
        gate_sb = sb("gate_sb", [P, DK, E])
        mods = sb("mods", [P, B, 4, D])
        mod_cols = sb("mod_cols", [P, 4, B])
        h2x = sb("h2x", [P, TT, 2, ROW])
        h2_cols = sb("h2_cols", [P, DK, P])
        zn = sb("zn", [P, NH, HD])
        zn_cols = sb("zn_cols", [P, DK, P])
        z_recip = sb("z_recip", [P, NH])
        ident = sb("ident", [P, P])
        identb = sb("identb", [P, P], BF16)
        causal = sb("causal", [P, P], BF16)
        earlier = sb("earlier", [P, P], BF16)
        onesb = sb("onesb", [P, P], BF16)
        c_sb = sb("c_sb", [B, D])
        c_cols = sb("c_cols", [P, DK, B])
        c_exp = sb("c_exp", [P, DK, B])
        c_silu = sb("c_silu", [P, DK, B])
        gtmp = sb("gtmp", [B, 2, D])
        stats = sb("stats", [P, TT, 6])
        moments = sb("moments", [P, TT, 2])
        rstd = sb("rstd", [P, TT])
        stats2 = sb("stats2", [P, 6])
        moments2 = sb("moments2", [P, 2, 2])
        rstd2 = sb("rstd2", [P, 2])
        minus_half = sb("minus_half", [P, TT])
        row_max = sb("row_max", [P, 2, TT, HU])
        max_parts = sb("max_parts", [HU, 3, T], BF16)
        max_rest = sb("max_rest", [HU, T])
        logits = sb("logits", [P, TT, E])
        gate_exp = sb("gate_exp", [P, TT, E])
        gate_p = sb("gate_p", [P, TT, E])
        gate_t = sb("gate_t", [P, TT, E])
        hot = sb("hot", [P, 2, TT, E])
        gate_s = sb("gate_s", [P, 4, TT])
        top_w = sb("top_w", [P, 2, TT])
        chosen = sb("chosen", [P, NT, E], BF16)
        before = sb("before", [P, NT + 1, E], BF16)
        rank_pos = sb("rank_pos", [P, TT, E])
        pos_f = sb("pos_f", [P, 2, TT])
        pos_i = sb("pos_i", [P, 2, TT], I32)
        rev_e = sb("rev_e", [P, E])
        base_e = sb("base_e", [P, E])
        part_base = sb("part_base", [P, E])
        dest = sb("dest", [P, 2, NT], I32)
        null_rows = sb("null_rows", [P, ROW])
        fill_f = sb("fill_f", [P, E])
        fill_i = sb("fill_i", [P, E], I32)
        count_f = sb("count_f", [1, E])
        count_i = sb("count_i", [1, E], I32)
        ntile = sb("ntile", [1, E])
        ends = sb("ends", [1, 4, E])
        tile_no = sb("tile_no", [1, TILES])
        tab_v = sb("tab_v", [1, 6, TILES])
        table = sb("table", [1, 2, TILES], I32)

        st = [ctx.enter_context(nc.psum_tensor(f"st{i}", [P, 2, 512], F32)) for i in range(2)]
        mx = [ctx.enter_context(nc.psum_tensor(f"mx{i}", [P, 512], F32)) for i in range(2)]
        pv = ctx.enter_context(nc.psum_tensor("pv", [P, 512], F32))
        misc = ctx.enter_context(nc.psum_tensor("misc", [P, 512], F32))

        x_loaded = [sem(f"x_loaded{b}") for b in range(B)]
        small_loaded = sem("small_loaded")
        wmod_loaded = sem("wmod_loaded")
        attn_w_loaded = sem("attn_w_loaded")
        first_w_loaded = sem("first_w_loaded")
        last_w_loaded = sem("last_w_loaded")
        pool_const = sem("pool_const")
        mod_ready = sem("mod_ready")
        mod_stored = sem("mod_stored")
        mods_loaded = sem("mods_loaded")
        c_step = sem("c_step")
        c_ready = sem("c_ready")
        setup_mm = sem("setup_mm")
        setup_dve = sem("setup_dve")
        wog_ready = sem("wog_ready")
        stats_ready = sem("stats_ready")
        rstd_ready = sem("rstd_ready")
        xn_ready = sem("xn_ready")
        misc_filled = sem("misc_filled")
        act_evac = sem("act_evac")
        dve_evac = sem("dve_evac")
        high_ready = sem("high_ready")
        mid_ready = sem("mid_ready")
        low_ready = sem("low_ready")
        parts_stored = [sem(f"parts_stored{w}") for w in range(2)]
        stack_loaded = [sem(f"stack_loaded{i}") for i in range(STACKS)]
        mx_filled = sem("mx_filled")
        mx_drained = sem("mx_drained")
        mhigh_ready = sem("mhigh_ready")
        mmid_ready = sem("mmid_ready")
        mlow_ready = sem("mlow_ready")
        max_stored = sem("max_stored")
        max_loaded = [sem(f"max_loaded{i}") for i in range(STACKS)]
        st_filled = sem("st_filled")
        exp_done = sem("exp_done")
        masked = sem("masked")
        pv_done = sem("pv_done")
        z_copied = sem("z_copied")
        stats2_ready = sem("stats2_ready")
        rstd2_ready = sem("rstd2_ready")
        xn2_ready = sem("xn2_ready")
        h2_ready = sem("h2_ready")
        h2_copied = sem("h2_copied")
        shifted = sem("shifted")
        gate_exped = sem("gate_exped")
        chosen_ready = sem("chosen_ready")
        routed = sem("routed")
        scattered = sem("scattered")
        fill_ready = sem("fill_ready")
        table_ready = sem("table_ready")
        null_stored = sem("null_stored")
        vec_step = sem("vec_step")
        pool_step = sem("pool_step")
        xg_loaded = sem("xg_loaded")
        xg_turned = sem("xg_turned")
        xg_copied = sem("xg_copied")
        gate_mm = sem("gate_mm")
        up_mm = sem("up_mm")
        silu_done = sem("silu_done")
        hidden_ready = sem("hidden_ready")
        hidden_turned = sem("hidden_turned")
        hidden_copied = sem("hidden_copied")
        y_mm = sem("y_mm")
        y_copied = sem("y_copied")
        y_stored = sem("y_stored")
        store_turn = sem("store_turn")
        y_loaded = sem("y_loaded")
        out_ready = sem("out_ready")
        out_stored = sem("out_stored")

        STEPS = attention_steps()
        ON_ACT = ("h_cols", "values", "z_cols", "h2_cols", "router")
        ON_DVE = ("project", "max_rows", "z_rows", "out_rows", "rank")
        use, evacs = {}, {"act": 0, "dve": 0}
        for key in STEPS:
            if key[0] in ON_ACT + ON_DVE:
                who = "act" if key[0] in ON_ACT else "dve"
                evacs[who] += 1
                use[key] = (len(use), who, evacs[who])
        use_order = sorted(use, key=lambda k: use[k][0])

        def wait_filled(eng, key):
            eng.wait_ge(misc_filled, use[key][0] + 1)

        def wait_evacuated(eng, key):
            _, who, count = use[key]
            eng.wait_ge(act_evac if who == "act" else dve_evac, count)

        def stack_turn(u):
            return u // STACKS + 1

        block = ctx.enter_context(nc.Block())

        @block.sync
        def _(sp):
            sp.dma_start(c_sb[:, :], c).then_inc(small_loaded, 16)
            xv = x.rearrange("b (i p) d -> b p i d", p=P)
            sp.dma_start(xs[:, 0:TT, :], xv[0]).then_inc(x_loaded[0], 16)
            sp.dma_start(wmod_sb, wmod.rearrange("(j p) n -> p j n", p=P)).then_inc(wmod_loaded, 16)
            for n, w in enumerate((wq, wk)):
                sp.dma_start(wqk_sb[:, n], w.rearrange("(j p) n -> p j n", p=P)).then_inc(attn_w_loaded, 16)
            sp.dma_start(wv_sb[:, :, :], wv.rearrange("(j p) n -> p j n", p=P)).then_inc(attn_w_loaded, 16)
            sp.dma_start(wo_sb[:, :, :], wo.rearrange("(j p) n -> p j n", p=P)).then_inc(attn_w_loaded, 16)
            sp.dma_start(gate_sb[:, :, :], gate_w.rearrange("(j p) n -> p j n", p=P)).then_inc(attn_w_loaded, 16)
            sp.wait_ge(mod_ready, 1)
            sp.dma_start(mod_dram[:, :], mod_rows).then_inc(mod_stored, 16)
            for b in range(1, B):
                sp.dma_start(xs[:, b * TT:(b + 1) * TT, :], xv[b]).then_inc(x_loaded[b], 16)
            sp.wait_ge(mod_stored, 16)
            sp.dma_start(mods[:, :, :, :].rearrange("p b m d -> p b (m d)"),
                         mod_dram[:, 2 * D:6 * D].partition_broadcast(P)).then_inc(mods_loaded, 16)

            def load_weights(e, done):
                sp.dma_start(weights[:, e, W1:W3].rearrange("p (j f) -> p j f", j=DK),
                             w1[e].rearrange("(j p) f -> p j f", p=P)).then_inc(done, 16)
                sp.dma_start(weights[:, e, W3:W2].rearrange("p (j f) -> p j f", j=DK),
                             w3[e].rearrange("(j p) f -> p j f", p=P)).then_inc(done, 16)
                sp.dma_start(weights[:, e, W2:WCOLS].rearrange("p (j d) -> p j d", j=FK),
                             w2[e].rearrange("(j p) d -> p j d", p=P)).then_inc(done, 16)

            sp.wait_ge(pool_const, 1)
            sp.dma_start(routed_dram[NULL_ROW:NULL_ROW + P, :], null_rows[:, :]).then_inc(null_stored, 16)

            early = 0
            for key in STEPS:
                if key[0] == "split":
                    _, u, w = key
                    sp.wait_ge(low_ready, 2 * u + w + 1)
                    sp.dma_start(split_dram[u, w], parts[w]).then_inc(parts_stored[w], 16)
                    sp.wait_ge(parts_stored[w], 16 * (u + 1))
                    if u >= STACKS:
                        sp.wait_ge(st_filled, 12 * (u - STACKS + 1))
                    stack = (q_stack, k_stack)[w][u % STACKS]
                    for g in range(NTERMS):
                        part = (Q_PART, K_PART)[w][g]
                        src = split_dram[u, w, :, part, :].rearrange("(h d) t -> d h t", d=HD)
                        sp.dma_start(stack[g * HD:(g + 1) * HD, :, :], src).then_inc(stack_loaded[u % STACKS], 16)
                    if early < EARLY and w == 1:
                        load_weights(early, first_w_loaded)
                        early += 1
                if key[0] == "max_split":
                    u = key[1]
                    sp.wait_ge(mlow_ready, u + 1)
                    sp.dma_start(max_dram[u], max_parts[:, :, :]).then_inc(max_stored, 16)
                    sp.wait_ge(max_stored, 16 * (u + 1))
                    sp.dma_start(q_stack[u % STACKS][KS:KB, :, :],
                                 max_dram[u].rearrange("h a t -> a h t")).then_inc(max_loaded[u % STACKS], 16)
            wait_filled(sp, ("z_rows", NT - 1))
            for e in range(EARLY, E):
                load_weights(e, last_w_loaded)
            sp.wait_ge(table_ready, 1)
            sp.wait_ge(scattered, 16 * (2 * NT + E))
            sp.wait_ge(null_stored, 16)

            def load_rows(k, first=False):
                row = sp.value_load(table[0:1, 1, bass.ds(k, 1)], min_val=0, max_val=NULL_ROW)
                if not first:
                    sp.wait_ge(xg_copied, 2 * k)
                sp.dma_start(xg, routed_dram[bass.ds(row, P), :]).then_inc(xg_loaded, 16)

            load_rows(0, first=True)
            with sp.Fori(1, TILES) as k:
                load_rows(k)
            sp.wait_ge(y_stored, 16 * TILES)
            sp.dma_start(ya, expert_dram[0:N, :].rearrange("(t p) d -> p t d", p=P)).then_inc(y_loaded, 16)
            sp.dma_start(yb, expert_dram[N:2 * N, :].rearrange("(t p) d -> p t d", p=P)).then_inc(y_loaded, 16)
            outv = out.rearrange("b (i p) d -> b p i d", p=P)
            for b in range(B):
                sp.wait_ge(out_ready, b + 1)
                sp.dma_start(outv[b], xs[:, b * TT:(b + 1) * TT, :]).then_inc(out_stored, 16)
            sp.wait_ge(out_stored, 16 * B)

        @block.gpsimd
        def _(pool):
            steps = [0]

            def own(ins):
                steps[0] += 1
                ins.then_inc(pool_step, 1)
                pool.wait_ge(pool_step, steps[0])

            consts = [0]

            def const(ins):
                consts[0] += 1
                ins.then_inc(pool_const, 1)
                pool.wait_ge(pool_const, consts[0])

            own(pool.memset(null_rows[:, :], 0.0))
            const(pool.iota(null_rows[:, DEST:DEST + 1].bitcast(I32), pattern=[[0, 1]], base=2 * N,
                      channel_multiplier=1))
            own(pool.memset(ident[:, :], 0.0))
            own(pool.affine_select(out=ident[:, :], in_=ident[:, :], compare_op=ALU.not_equal, fill=1.0, base=0,
                                   pattern=[[-1, P]], channel_multiplier=1))
            const(pool.tensor_copy(identb[:, :], ident[:, :]))
            own(pool.memset(causal[:, :], 0.0))
            const(pool.affine_select(out=causal[:, :], in_=causal[:, :], compare_op=ALU.is_ge, fill=NEG, base=0,
                               pattern=[[-1, P]], channel_multiplier=1))
            own(pool.memset(earlier[:, :], 1.0))
            const(pool.affine_select(out=earlier[:, :], in_=earlier[:, :], compare_op=ALU.is_gt, fill=0.0, base=0,
                               pattern=[[1, P]], channel_multiplier=-1))
            const(pool.memset(onesb[:, :], 1.0))
            const(pool.memset(minus_half[:, :], -0.5))
            for s in range(STACKS):
                const(pool.memset(k_stack[s][96:128, :, :], 1.0))
            for s in range(2):
                own(pool.memset(v_rows[s], 0.0))
                const(pool.memset(v_rows[s][:, :, :, HD:HD + 1], 1.0))
            const(pool.iota(rev_e[:, :], pattern=[[-1, E]], base=E, channel_multiplier=0,
                      allow_small_or_imprecise_dtypes=True))
            const(pool.iota(base_e[:, :], pattern=[[REGION, E]], base=0, channel_multiplier=0,
                      allow_small_or_imprecise_dtypes=True))
            const(pool.iota(part_base[:, :], pattern=[[REGION, E]], base=0, channel_multiplier=1,
                      allow_small_or_imprecise_dtypes=True))
            const(pool.iota(dest[:, :, :], pattern=[[N, 2], [P, NT]], base=0, channel_multiplier=1))
            const(pool.iota(tile_no[:, :], pattern=[[1, TILES]], base=0, channel_multiplier=0,
                      allow_small_or_imprecise_dtypes=True))
            const(pool.memset(before[:, 0, :], 0.0))

            for key in STEPS:
                kind = key[0]
                if kind == "norm_stats":
                    b = key[1]
                    pool.wait_ge(stats_ready, b + 1)
                    own(pool.tensor_scalar(rstd[:, :], moments[:, :, 1], EPS, None, ALU.add))
                    pool.tensor_tensor(rstd[:, :], rstd[:, :], minus_half[:, :], ALU.pow).then_inc(rstd_ready, 1)
                elif kind == "split":
                    _, u, w = key
                    n = 2 * u + w
                    pool.wait_ge(mid_ready, n + 1)
                    pool.tensor_tensor(parts[w][:, 2, :], rest[w], parts[w][:, 1, :], ALU.subtract).then_inc(low_ready, 1)
                elif kind == "max_split":
                    u = key[1]
                    pool.wait_ge(mmid_ready, u + 1)
                    pool.tensor_tensor(max_parts[:, 2, :], max_rest[:, :], max_parts[:, 1, :],
                                       ALU.subtract).then_inc(mlow_ready, 1)
                elif kind == "score":
                    _, g, n = key
                    k, h0, nh = score_slot(n)
                    if h0 + nh == HG:
                        pool.wait_ge(exp_done, 6 * g + n + 1)
                        diag = probs[k][:, :, 0:P]
                        pool.affine_select(out=diag, in_=diag, compare_op=ALU.is_ge, fill=0.0, base=0,
                                           pattern=[[0, HG], [1, P]], channel_multiplier=-1).then_inc(masked, 1)
                elif kind == "z_rows" and key[1] % TT == 0:
                    b = key[1] // TT
                    if b == 0:
                        pool.wait_ge(mods_loaded, 16)
                        pool.wait_ge(attn_w_loaded, 80)
                    else:
                        wait_filled(pool, ("out_rows", b * TT - 1))
                    pool.tensor_tensor(wog[:, :, :], wo_sb[:, :, :],
                                       mods[:, b, 0, :].unsqueeze(1).to_broadcast([P, DK, D]), ALU.mult).then_inc(wog_ready, 1)
                elif kind == "out_rows":
                    t = key[1]
                    pool.wait_ge(stats2_ready, t + 1)
                    own(pool.tensor_scalar(rstd2[:, t % 2:t % 2 + 1], moments2[:, t % 2, 1:2], EPS, None, ALU.add))
                    pool.tensor_tensor(rstd2[:, t % 2:t % 2 + 1], rstd2[:, t % 2:t % 2 + 1], minus_half[:, 0:1],
                                       ALU.pow).then_inc(rstd2_ready, 1)
                elif kind == "norm2":
                    t = key[1]
                    b, i = t // TT, t % TT
                    row = h2x[:, i, 0, 0:D]
                    pool.wait_ge(xn2_ready, t + 1)
                    own(pool.tensor_tensor(row, row, mods[:, b, 2, :], ALU.mult))
                    pool.tensor_tensor(row, row, mods[:, b, 1, :], ALU.add).then_inc(h2_ready, 1)
                elif kind == "scatter":
                    b = key[1]
                    pool.wait_ge(routed, b + 1)
                    pool.wait_ge(h2_copied, (b + 1) * TT)
                    for i in range(TT):
                        for n in range(2):
                            pool.indirect_dma_start(
                                out=routed_dram[:, :], out_offset=bass.IndirectOffsetOnAxis(ap=pos_i[:, n, i:i + 1], axis=0),
                                in_=h2x[:, i, n, :], in_offset=None).then_inc(scattered, 16)
            pool.wait_ge(fill_ready, 1)
            for e in range(E):
                pool.indirect_dma_start(
                    out=routed_dram[:, :], out_offset=bass.IndirectOffsetOnAxis(ap=fill_i[:, e:e + 1], axis=0),
                    in_=null_rows[:, :], in_offset=None).then_inc(scattered, 16)

            def store_rows(k, parity):
                pool.wait_ge(y_copied, k + 1)
                pool.sem_inc(store_turn, 1)
                pool.indirect_dma_start(
                    out=expert_dram[:, :],
                    out_offset=bass.IndirectOffsetOnAxis(ap=tail[parity][:, 0:1].bitcast(I32), axis=0),
                    in_=y_rows, in_offset=None).then_inc(y_stored, 16)

            store_rows(0, 0)
            with pool.Fori(1, TILES - 2, 2) as k:
                store_rows(k, 1)
                store_rows(k + 1, 0)
            store_rows(TILES - 2, 1)
            store_rows(TILES - 1, 0)

        @block.scalar
        def _(act):
            act.wait_ge(setup_dve, 1)
            act.activation(c_exp[:, :, :], c_cols[:, :, :], ACT.Exp, scale=-1.0).then_inc(c_step, 1)
            for key in STEPS:
                kind = key[0]
                if kind == "h_cols":
                    _, b, j = key
                    act.wait_ge(setup_dve, 5)
                    wait_filled(act, key)
                    act.activation(h_cols[b % 2][:, j, :], misc[:, :], ACT.Identity,
                                   bias=mod_cols[:, j, b:b + 1], scale=mod_cols[:, 2 + j, b:b + 1]).then_inc(act_evac, 1)
                elif kind == "values":
                    _, b, i = key
                    act.wait_ge(pool_const, 11)
                    wait_filled(act, key)
                    act.activation(v_rows[b % 2][:, i, :, 0:HD], misc[:, 0:D].rearrange("p (h d) -> p h d", h=NH),
                                   ACT.Copy).then_inc(act_evac, 1)
                elif kind == "project":
                    _, u, w = key
                    wait_filled(act, key)
                    if u >= 1:
                        act.wait_ge(parts_stored[w], 16 * u)
                    act.activation(parts[w][:, 0, :], misc[:, :], ACT.Copy,
                                   scale=(HD ** -0.5, 1.0)[w]).then_inc(high_ready, 1)
                elif kind == "split":
                    _, u, w = key
                    wait_evacuated(act, ("project", u, w))
                    act.activation(parts[w][:, 1, :], rest[w], ACT.Copy).then_inc(mid_ready, 1)
                elif kind == "max_rows":
                    u = key[1]
                    wait_filled(act, key)
                    if u >= 1:
                        act.wait_ge(max_stored, 16 * u)
                    act.activation(max_parts[:, 0, :], misc[0:HU, :], ACT.Copy, scale=-1.0).then_inc(mhigh_ready, 1)
                elif kind == "max_split":
                    u = key[1]
                    wait_evacuated(act, ("max_rows", u))
                    act.activation(max_parts[:, 1, :], max_rest[:, :], ACT.Copy).then_inc(mmid_ready, 1)
                elif kind == "score":
                    _, g, n = key
                    k, h0, nh = score_slot(n)
                    w = T - k * P
                    s = 6 * g + n
                    if s == 0:
                        act.wait_ge(mod_stored, 16)
                    if g >= 1:
                        act.wait_ge(pv_done, 4 * (g - 1) + k + 1)
                    act.wait_ge(st_filled, s + 1)
                    if k < 2:
                        src = st[s % 2][:, 0:nh, 0:w]
                    else:
                        src = st[s % 2][:, :, :].rearrange("p a (b t) -> p (a b) t", t=w)[:, 0:nh, :]
                    act.activation(probs[k][:, h0:h0 + nh, :], src, ACT.Exp).then_inc(exp_done, 1)
                elif kind == "value_sum":
                    _, g, k = key
                    if k == TT - 1:
                        act.wait_ge(pv_done, 4 * (g + 1))
                        if g >= 8:
                            wait_filled(act, ("z_rows", (g // 4 - 1) * TT - 1))
                        act.activation(z_cols[g // 4 % 2][:, g % 4, :], pv[:, :], ACT.Copy).then_inc(z_copied, 1)
                elif kind == "z_cols":
                    wait_filled(act, key)
                    act.activation(zn_cols[:, :, :].rearrange("p j t -> p (j t)"), misc[:, 0:D], ACT.Copy).then_inc(act_evac, 1)
                elif kind == "h2_cols":
                    t = key[1]
                    wait_filled(act, key)
                    act.activation(h2_cols[:, :, :].rearrange("p j t -> p (j t)"), misc[:, 0:D], ACT.Copy).then_inc(act_evac, 1)
                    act.activation(h2x[:, t % TT, 1, 0:D], h2x[:, t % TT, 0, 0:D], ACT.Copy).then_inc(h2_copied, 1)
                elif kind == "router":
                    t = key[1]
                    wait_filled(act, key)
                    if t >= TT:
                        act.wait_ge(shifted, t // TT)
                    act.activation(logits[:, t % TT, :], misc[:, 0:E], ACT.Copy).then_inc(act_evac, 1)
                elif kind == "gate":
                    b = key[1]
                    act.wait_ge(shifted, b + 1)
                    act.activation(gate_exp[:, :, :], gate_t[:, :, :], ACT.Exp).then_inc(gate_exped, 1)

            def silu(k):
                act.wait_ge(gate_mm, k + 1)
                act.activation(silu_sb, mx[0][:, :], ACT.Silu).then_inc(silu_done, 1)

            def hidden_out(k):
                act.wait_ge(hidden_turned, k + 1)
                act.activation(hidden_cols.rearrange("p j t -> p (j t)"), pv[:, :], ACT.Copy).then_inc(hidden_copied, 1)

            def y_out(k, parity, first=False):
                if not first:
                    act.wait_ge(y_stored, 16 * k)
                act.wait_ge(y_mm, k + 1)
                act.activation(y_rows, st[0][:, 0, 0:D], ACT.Copy, scale=tail[parity][:, 1:2]).then_inc(y_copied, 1)

            act.wait_ge(xg_copied, 2)
            silu(0)

            def tile(k, parity, first=False):
                hidden_out(k - 1)
                act.wait_ge(hidden_ready, k)
                silu(k)
                y_out(k - 1, 1 - parity, first)

            tile(1, 1, first=True)
            with act.Fori(2, TILES - 1, 2) as k:
                tile(k, 0)
                tile(k + 1, 1)
            tile(TILES - 1, 0)
            hidden_out(TILES - 1)
            y_out(TILES - 1, 0)

        @block.tensor
        def _(pe):
            pe.wait_ge(small_loaded, 16)
            pe.wait_ge(pool_const, 2)
            for j in range(DK):
                ins = pe.transpose(misc[:, j * B:(j + 1) * B], c_sb[:, j * P:(j + 1) * P], ident[0:B, 0:B])
            ins.then_inc(setup_mm, 1)
            pe.wait_ge(c_ready, 1)
            pe.wait_ge(wmod_loaded, 16)
            for n, bank in enumerate((mx[0][0:B, :], mx[1][0:B, :], pv[0:B, :])):
                for j in range(DK):
                    ins = pe.matmul(bank, c_silu[:, j, :], wmod_sb[:, j, n * 512:(n + 1) * 512],
                                    start=(j == 0), stop=(j == DK - 1))
                ins.then_inc(setup_mm, 1)
            pe.wait_ge(mod_ready, 1)
            for n in range(4):
                ins = pe.transpose(misc[:, n * B:(n + 1) * B], mod_rows[:, n * P:(n + 1) * P], ident[0:B, 0:B])
            ins.then_inc(setup_mm, 1)
            pe.wait_ge(attn_w_loaded, 80)
            pe.wait_ge(pool_const, 17)
            pe.wait_ge(setup_dve, 5)

            for key in STEPS:
                kind = key[0]
                if key in use and use[key][0] > 0:
                    wait_evacuated(pe, use_order[use[key][0] - 1])
                if kind == "h_cols":
                    _, b, j = key
                    pe.wait_ge(xn_ready, TT * (b + 1))
                    for i in range(TT):
                        ins = pe.transpose(misc[:, i * P:(i + 1) * P], xn[:, i, j * P:(j + 1) * P], ident[:, :])
                    ins.then_inc(misc_filled, 1)
                elif kind == "values":
                    _, b, i = key
                    wait_evacuated(pe, ("h_cols", b, 1))
                    for j in range(DK):
                        ins = pe.matmul(misc[:, 0:D], h_cols[b % 2][:, j, i * P:(i + 1) * P], wv_sb[:, j, :],
                                        start=(j == 0), stop=(j == DK - 1))
                    ins.then_inc(misc_filled, 1)
                elif kind == "project":
                    _, u, w = key
                    b, half = u // 2, u % 2
                    wait_evacuated(pe, ("h_cols", b, 1))
                    for j in range(DK):
                        ins = pe.matmul(misc[:, :], wqk_sb[:, w, j, half * P:(half + 1) * P], h_cols[b % 2][:, j, :],
                                        start=(j == 0), stop=(j == DK - 1))
                    ins.then_inc(misc_filled, 1)
                elif kind == "max_fill":
                    _, u, n = key
                    i, h0, nh = max_fill(n)
                    w = (i + 1) * P
                    f = 22 * u + n
                    if n == 0:
                        pe.wait_ge(stack_loaded[u % STACKS], 16 * 2 * NTERMS * stack_turn(u))
                    if f >= 2:
                        pe.wait_ge(mx_drained, f - 1)
                    bank = mx[f % 2]
                    qs, ks = q_stack[u % STACKS], k_stack[u % STACKS]
                    for a in range(nh):
                        pe.matmul(bank[:, a * w:(a + 1) * w], qs[0:KS, h0 + a, i * P:(i + 1) * P], ks[0:KS, h0 + a, 0:w],
                                  start=(a == 0), stop=False, skip_group_check=True)
                    diag = bank[:, 0:nh * w].rearrange("p (h s) -> p h s", h=nh)[:, :, i * P:(i + 1) * P]
                    pe.matmul(diag, identb[:, :], causal[:, :].unsqueeze(1).to_broadcast([P, nh, P]),
                              start=False, stop=True, skip_group_check=True).then_inc(mx_filled, 1)
                elif kind == "max_rows":
                    u = key[1]
                    pe.wait_ge(mx_drained, 22 * (u + 1))
                    for i in range(TT):
                        ins = pe.transpose(misc[0:HU, i * P:(i + 1) * P], row_max[:, u % 2, i, :], ident[:, :])
                    ins.then_inc(misc_filled, 1)
                elif kind == "score":
                    _, g, n = key
                    u = g // 2
                    k, h0, nh = score_slot(n)
                    w = T - k * P
                    s = 6 * g + n
                    if s >= 2:
                        pe.wait_ge(exp_done, s - 1)
                    if n == 0 and g % 2 == 0:
                        pe.wait_ge(max_loaded[u % STACKS], 16 * stack_turn(u))
                    qs, ks = q_stack[u % STACKS], k_stack[u % STACKS]
                    for a in range(nh):
                        h = (g % 2) * HG + h0 + a
                        if k < 2:
                            dst, first, last = st[s % 2][:, a, 0:w], True, True
                        else:
                            per = 512 // w
                            dst = st[s % 2][:, a // per, (a % per) * w:(a % per + 1) * w]
                            first, last = a % per == 0, a % per == per - 1
                        ins = pe.matmul(dst, ks[0:KB, h, k * P:(k + 1) * P], qs[0:KB, h, k * P:T],
                                        start=first, stop=last, skip_group_check=True)
                    ins.then_inc(st_filled, 1)
                elif kind == "value_sum":
                    _, g, k = key
                    b = g // 4
                    pe.wait_ge(masked, 4 * g + k + 1)
                    if k == 0:
                        wait_evacuated(pe, ("values", b, TT - 1))
                        if g >= 1:
                            pe.wait_ge(z_copied, g)
                    for a in range(HG):
                        h = (g % 4) * HG + a
                        ins = pe.matmul(pv[32 * a:32 * a + 32, k * P:T], v_rows[b % 2][:, k, h, :], probs[k][:, a, :],
                                        start=(k == 0), stop=(k == TT - 1), skip_group_check=True)
                    ins.then_inc(pv_done, 1)
                elif kind == "z_rows":
                    t = key[1]
                    b, i = t // TT, t % TT
                    pe.wait_ge(z_copied, 4 * (b + 1))
                    for g in range(4):
                        ins = pe.transpose(misc[:, g * P:(g + 1) * P], z_cols[b % 2][:, g, i * P:(i + 1) * P], ident[:, :])
                    ins.then_inc(misc_filled, 1)
                elif kind == "z_cols":
                    t = key[1]
                    wait_evacuated(pe, ("z_rows", t))
                    for j in range(DK):
                        ins = pe.transpose(misc[:, j * P:(j + 1) * P],
                                           zn[:, j * HU:(j + 1) * HU, :].rearrange("p h d -> p (h d)"), ident[:, :])
                    ins.then_inc(misc_filled, 1)
                elif kind == "out_rows":
                    t = key[1]
                    wait_evacuated(pe, ("z_cols", t))
                    pe.wait_ge(wog_ready, t // TT + 1)
                    for j in range(DK):
                        ins = pe.matmul(misc[:, 0:D], zn_cols[:, j, :], wog[:, j, :], start=(j == 0), stop=(j == DK - 1))
                    ins.then_inc(misc_filled, 1)
                elif kind == "h2_cols":
                    t = key[1]
                    pe.wait_ge(h2_ready, t + 1)
                    for j in range(DK):
                        ins = pe.transpose(misc[:, j * P:(j + 1) * P], h2x[:, t % TT, 0, j * P:(j + 1) * P], ident[:, :])
                    ins.then_inc(misc_filled, 1)
                elif kind == "router":
                    t = key[1]
                    wait_evacuated(pe, ("h2_cols", t))
                    for j in range(DK):
                        ins = pe.matmul(misc[:, 0:E], h2_cols[:, j, :], gate_sb[:, j, :], start=(j == 0), stop=(j == DK - 1))
                    ins.then_inc(misc_filled, 1)
                elif kind == "rank":
                    b = key[1]
                    pe.wait_ge(chosen_ready, b + 1)
                    for i in range(TT):
                        t = b * TT + i
                        pe.matmul(misc[:, i * E:(i + 1) * E], earlier[:, :], chosen[:, t, :],
                                  start=(i == 0), stop=False, skip_group_check=True)
                        ins = pe.matmul(misc[:, i * E:(i + 1) * E], onesb[:, :], before[:, t, :],
                                        start=False, stop=(i == TT - 1), skip_group_check=True)
                    ins.then_inc(misc_filled, 1)
            wait_evacuated(pe, use_order[-1])
            pe.matmul(misc[:, 0:E], onesb[:, :], before[:, NT, :], start=True, stop=True).then_inc(setup_mm, 1)

            pe.wait_ge(first_w_loaded, 16 * 3 * EARLY)
            pe.wait_ge(last_w_loaded, 16 * 3 * (E - EARLY))
            pe.wait_ge(table_ready, 1)
            pe.wait_ge(exp_done, 6 * GROUPS)
            pe.wait_ge(z_copied, GROUPS)
            pe.wait_ge(mx_drained, 22 * UNITS)

            def expert_of(k):
                return pe.value_load(table[0:1, 0, bass.ds(k, 1)], min_val=0, max_val=E - 1)

            def turn_rows(k):
                pe.wait_ge(xg_loaded, 16 * (k + 1))
                for j in range(DK):
                    ins = pe.transpose(misc[:, j * P:(j + 1) * P], xg[:, j * P:(j + 1) * P], ident[:, :])
                ins.then_inc(xg_turned, 1)

            def up(k, e, col, bank, done):
                for j in range(DK):
                    w = arena[:, bass.ds(e * WCOLS + (col + j * F), F)]
                    ins = pe.matmul(bank[:, :], xg_cols[:, j, :], w, start=(j == 0), stop=(j == DK - 1))
                ins.then_inc(done, 1)

            def turn_hidden(k):
                pe.wait_ge(hidden_ready, k + 1)
                for j in range(FK):
                    ins = pe.transpose(pv[:, j * P:(j + 1) * P], hidden[:, j * P:(j + 1) * P], ident[:, :])
                ins.then_inc(hidden_turned, 1)

            def down(k, e, first=False):
                pe.wait_ge(hidden_copied, k + 1)
                if not first:
                    pe.wait_ge(y_copied, k)
                for j in range(FK):
                    w = arena[:, bass.ds(e * WCOLS + (W2 + j * D), D)]
                    ins = pe.matmul(st[0][:, 0, 0:D], hidden_cols[:, j, :], w, start=(j == 0), stop=(j == FK - 1))
                ins.then_inc(y_mm, 1)

            def tile(k, first=False):
                e, e_before = expert_of(k), expert_of(k - 1)
                pe.wait_ge(xg_copied, 2 * (k + 1))
                up(k, e, W1, mx[0], gate_mm)
                turn_hidden(k - 1)
                return e, e_before

            turn_rows(0)
            pe.wait_ge(xg_copied, 2)
            e0 = expert_of(0)
            up(0, e0, W1, mx[0], gate_mm)
            turn_rows(1)
            up(0, e0, W3, mx[1], up_mm)

            def middle(k, first=False):
                e, e_before = tile(k)
                turn_rows(k + 1)
                up(k, e, W3, mx[1], up_mm)
                down(k - 1, e_before, first)

            middle(1, first=True)
            with pe.Fori(2, TILES - 1) as k:
                middle(k)
            e, e_before = tile(TILES - 1)
            up(TILES - 1, e, W3, mx[1], up_mm)
            down(TILES - 2, e_before)
            turn_hidden(TILES - 1)
            down(TILES - 1, e)

        @block.vector
        def _(dve):
            steps = [0]

            def own(ins):
                steps[0] += 1
                ins.then_inc(vec_step, 1)
                dve.wait_ge(vec_step, steps[0])

            dve.wait_ge(setup_mm, 1)
            dve.tensor_copy(c_cols[:, :, :].rearrange("p j b -> p (j b)"), misc[:, 0:DK * B]).then_inc(setup_dve, 1)
            dve.wait_ge(c_step, 1)
            own(dve.tensor_scalar(c_exp[:, :, :], c_exp[:, :, :], 1.0, None, ALU.add))
            own(dve.reciprocal(c_silu[:, :, :], c_exp[:, :, :]))
            dve.tensor_tensor(c_silu[:, :, :], c_silu[:, :, :], c_cols[:, :, :], ALU.mult).then_inc(c_ready, 1)
            dve.wait_ge(setup_mm, 4)
            dve.tensor_copy(mod_rows[:, 0:D], mx[0][0:B, 0:D]).then_inc(setup_dve, 1)
            dve.tensor_scalar(mod_rows[:, D:2 * D], mx[0][0:B, D:2 * D], 1.0, None, ALU.add).then_inc(setup_dve, 1)
            dve.tensor_scalar(mod_rows[:, 4 * D:5 * D], pv[0:B, 0:D], 1.0, None, ALU.add).then_inc(setup_dve, 1)
            own(dve.tensor_copy(mod_rows[:, 3 * D:4 * D], mx[1][0:B, D:2 * D]))
            for n, src in enumerate((mx[1][0:B, 0:D], pv[0:B, D:2 * D])):
                own(dve.tensor_scalar(gtmp[:, 0, :], src, 0.0, 2.0, ALU.is_ge, ALU.mult))
                own(dve.tensor_scalar(gtmp[:, 0, :], gtmp[:, 0, :], -1.0, None, ALU.add))
                own(dve.tensor_scalar(gtmp[:, 1, :], src, -1.0, None, ALU.mult))
                own(dve.tensor_tensor(gtmp[:, 1, :], gtmp[:, 1, :], src, ALU.max))
                own(dve.tensor_scalar(gtmp[:, 1, :], gtmp[:, 1, :], 0.25, None, ALU.max))
                ins = dve.tensor_tensor(mod_rows[:, (2 + 3 * n) * D:(3 + 3 * n) * D], gtmp[:, 0, :], gtmp[:, 1, :], ALU.mult)
                if n == 0:
                    own(ins)
            ins.then_inc(mod_ready, 1)
            dve.wait_ge(setup_mm, 5)
            dve.tensor_copy(mod_cols[:, :, :].rearrange("p n b -> p (n b)"), misc[:, 0:4 * B]).then_inc(setup_dve, 1)

            for key in STEPS:
                kind = key[0]
                if kind == "norm_stats":
                    b = key[1]
                    dve.wait_ge(x_loaded[b], 16)
                    if b >= 1:
                        dve.wait_ge(rstd_ready, b)
                    for i in range(TT):
                        own(dve.bn_stats(stats[:, i, :], xs[:, b * TT + i, :]))
                        ins = dve.bn_aggr(moments[:, i, :], stats[:, i, :])
                        if i < TT - 1:
                            own(ins)
                    ins.then_inc(stats_ready, 1)
                elif kind == "norm_rows":
                    b = key[1]
                    dve.wait_ge(rstd_ready, b + 1)
                    if b >= 1:
                        wait_filled(dve, ("h_cols", b - 1, 1))
                    for i in range(TT):
                        dve.tensor_scalar(xn[:, i, :], xs[:, b * TT + i, :], moments[:, i, 0:1], rstd[:, i:i + 1],
                                          ALU.subtract, ALU.mult).then_inc(xn_ready, 1)
                elif kind == "project":
                    _, u, w = key
                    n = 2 * u + w
                    dve.wait_ge(high_ready, n + 1)
                    if n >= 2:
                        dve.wait_ge(low_ready, n - 1)
                    dve.scalar_tensor_tensor(out=rest[w], in0=misc[:, :], scalar=(HD ** -0.5, 1.0)[w],
                                             in1=parts[w][:, 0, :], op0=ALU.mult, op1=ALU.subtract).then_inc(dve_evac, 1)
                elif kind == "max_fill":
                    _, u, n = key
                    i, h0, nh = max_fill(n)
                    w = (i + 1) * P
                    f = 22 * u + n
                    if n == 0 and u >= 2:
                        wait_filled(dve, ("max_rows", u - 2))
                    dve.wait_ge(mx_filled, f + 1)
                    dve.tensor_reduce(row_max[:, u % 2, i, h0:h0 + nh],
                                      mx[f % 2][:, 0:nh * w].rearrange("p (h s) -> p h s", h=nh), AX_X, ALU.max).then_inc(mx_drained, 1)
                elif kind == "max_rows":
                    u = key[1]
                    dve.wait_ge(mhigh_ready, u + 1)
                    if u >= 1:
                        dve.wait_ge(mlow_ready, u)
                    dve.scalar_tensor_tensor(out=max_rest[:, :], in0=misc[0:HU, :], scalar=-1.0,
                                             in1=max_parts[:, 0, :], op0=ALU.mult, op1=ALU.subtract).then_inc(dve_evac, 1)
                elif kind == "z_rows":
                    t = key[1]
                    wait_filled(dve, key)
                    z = misc[:, :].rearrange("p (h d) -> p h d", h=NH)
                    own(dve.reciprocal(z_recip[:, :], z[:, :, HD]))
                    dve.tensor_tensor(zn[:, :, :], z[:, :, 0:HD], z_recip[:, :].unsqueeze(2).to_broadcast([P, NH, HD]),
                                      ALU.mult).then_inc(dve_evac, 1)
                elif kind == "out_rows":
                    t = key[1]
                    wait_filled(dve, key)
                    dve.tensor_tensor(xs[:, t, :], misc[:, 0:D], xs[:, t, :], ALU.add).then_inc(dve_evac, 1)
                    wait_evacuated(dve, key)
                    if t >= 2:
                        dve.wait_ge(rstd2_ready, t - 1)
                    own(dve.bn_stats(stats2[:, :], xs[:, t, :]))
                    dve.bn_aggr(moments2[:, t % 2, :], stats2[:, :]).then_inc(stats2_ready, 1)
                elif kind == "norm2":
                    t = key[1]
                    b, i = t // TT, t % TT
                    dve.wait_ge(rstd2_ready, t + 1)
                    if i == 0 and b >= 1:
                        dve.wait_ge(scattered, 16 * 2 * TT * b)
                    dve.tensor_scalar(h2x[:, i, 0, 0:D], xs[:, t, :], moments2[:, t % 2, 0:1], rstd2[:, t % 2:t % 2 + 1],
                                      ALU.subtract, ALU.mult).then_inc(xn2_ready, 1)
                elif kind == "gate":
                    b = key[1]
                    wait_evacuated(dve, ("router", b * TT + TT - 1))
                    own(dve.tensor_reduce(gate_s[:, 0, :], logits[:, :, :], AX_X, ALU.max))
                    dve.tensor_tensor(gate_t[:, :, :], logits[:, :, :], gate_s[:, 0, :].unsqueeze(2).to_broadcast([P, TT, E]),
                                      ALU.subtract).then_inc(shifted, 1)
                elif kind == "choose":
                    b = key[1]
                    wide = [P, TT, E]
                    rev = rev_e[:, :].unsqueeze(1).to_broadcast(wide)
                    dve.wait_ge(gate_exped, b + 1)
                    own(dve.tensor_reduce(gate_s[:, 1, :], gate_exp[:, :, :], AX_X, ALU.add))
                    own(dve.reciprocal(gate_s[:, 2, :], gate_s[:, 1, :]))
                    own(dve.tensor_tensor(gate_p[:, :, :], gate_exp[:, :, :], gate_s[:, 2, :].unsqueeze(2).to_broadcast(wide), ALU.mult))
                    for n in range(2):
                        own(dve.tensor_reduce(top_w[:, n, :], gate_p[:, :, :], AX_X, ALU.max))
                        own(dve.tensor_tensor(gate_t[:, :, :], gate_p[:, :, :], top_w[:, n, :].unsqueeze(2).to_broadcast(wide), ALU.is_equal))
                        own(dve.tensor_tensor(gate_t[:, :, :], gate_t[:, :, :], rev, ALU.mult))
                        own(dve.tensor_reduce(gate_s[:, 3, :], gate_t[:, :, :], AX_X, ALU.max))
                        own(dve.tensor_tensor(hot[:, n], rev, gate_s[:, 3, :].unsqueeze(2).to_broadcast(wide), ALU.is_equal))
                        if n == 0:
                            own(dve.scalar_tensor_tensor(out=gate_p[:, :, :], in0=hot[:, 0], scalar=-2.0, in1=gate_p[:, :, :],
                                                         op0=ALU.mult, op1=ALU.add))
                    own(dve.tensor_tensor(chosen[:, b * TT:(b + 1) * TT, :], hot[:, 0], hot[:, 1], ALU.add))
                    for i in range(TT):
                        t = b * TT + i
                        ins = dve.tensor_tensor(before[:, t + 1, :], before[:, t, :], chosen[:, t, :], ALU.add)
                        if i < TT - 1:
                            own(ins)
                    ins.then_inc(chosen_ready, 1)
                elif kind == "rank":
                    b = key[1]
                    wide = [P, TT, E]
                    wait_filled(dve, key)
                    dve.tensor_tensor(rank_pos[:, :, :], misc[:, 0:TT * E].rearrange("p (i e) -> p i e", i=TT),
                                      base_e[:, :].unsqueeze(1).to_broadcast(wide), ALU.add).then_inc(dve_evac, 1)
                    wait_evacuated(dve, key)
                    for n in range(2):
                        own(dve.tensor_tensor(gate_t[:, :, :], rank_pos[:, :, :], hot[:, n], ALU.mult))
                        own(dve.tensor_reduce(pos_f[:, n, :], gate_t[:, :, :], AX_X, ALU.add))
                        own(dve.tensor_copy(h2x[:, :, n, DEST].bitcast(I32), dest[:, n, b * TT:(b + 1) * TT]))
                        own(dve.tensor_copy(h2x[:, :, n, WEIGHT], top_w[:, n, :]))
                    dve.tensor_copy(pos_i[:, :, :], pos_f[:, :, :]).then_inc(routed, 1)
            dve.wait_ge(setup_mm, 6)
            own(dve.tensor_tensor(fill_f[:, :], misc[:, 0:E], part_base[:, :], ALU.add))
            own(dve.tensor_scalar(count_f[:, :], misc[0:1, 0:E], float(P - 1), None, ALU.add))
            dve.tensor_copy(fill_i[:, :], fill_f[:, :]).then_inc(fill_ready, 1)
            own(dve.tensor_copy(count_i[:, :], count_f[:, :]))
            own(dve.tensor_single_scalar(count_i[:, :], count_i[:, :], 7, ALU.logical_shift_right))
            own(dve.tensor_copy(ntile[:, :], count_i[:, :]))
            own(dve.tensor_copy(ends[:, 0, :], ntile[:, :]))
            for n, d in enumerate((1, 2, 4)):
                own(dve.tensor_copy(ends[:, n + 1, 0:d], ends[:, n, 0:d]))
                own(dve.tensor_tensor(ends[:, n + 1, d:E], ends[:, n, d:E], ends[:, n, 0:E - d], ALU.add))
            end = ends[:, 3, :]
            wide = [1, TILES, E]
            own(dve.tensor_tensor(tab_a, tile_no[:, :].unsqueeze(2).to_broadcast(wide),
                                  end.unsqueeze(1).to_broadcast(wide), ALU.is_ge))
            own(dve.tensor_tensor(tab_b, tab_a, ntile[:, :].unsqueeze(1).to_broadcast(wide), ALU.mult))
            own(dve.tensor_reduce(tab_v[:, 0, :], tab_a, AX_X, ALU.add))
            own(dve.tensor_reduce(tab_v[:, 1, :], tab_b, AX_X, ALU.add))
            own(dve.tensor_tensor(tab_v[:, 2, :], tile_no[:, :], tab_v[:, 1, :], ALU.subtract))
            own(dve.tensor_scalar(tab_v[:, 2, :], tab_v[:, 2, :], float(P), None, ALU.mult))
            own(dve.scalar_tensor_tensor(out=tab_v[:, 3, :], in0=tab_v[:, 0, :], scalar=float(REGION), in1=tab_v[:, 2, :],
                                         op0=ALU.mult, op1=ALU.add))
            own(dve.tensor_scalar(tab_v[:, 3, :], tab_v[:, 3, :], float(NULL_ROW), None, ALU.min))
            own(dve.tensor_scalar(tab_v[:, 0, :], tab_v[:, 0, :], float(E - 1), None, ALU.min))
            own(dve.tensor_copy(table[:, 0, :], tab_v[:, 0, :]))
            dve.tensor_copy(table[:, 1, :], tab_v[:, 3, :]).then_inc(table_ready, 1)

            def rows_out(k, parity):
                dve.wait_ge(xg_turned, k + 1)
                dve.tensor_copy(xg_cols.rearrange("p j t -> p (j t)"), misc[:, 0:D]).then_inc(xg_copied, 1)
                dve.tensor_copy(tail[parity].bitcast(I32), xg[:, DEST:DEST + 2].bitcast(I32)).then_inc(xg_copied, 1)

            def gated(k):
                dve.wait_ge(silu_done, k + 1)
                dve.wait_ge(up_mm, k + 1)
                dve.tensor_tensor(hidden, silu_sb, mx[1][:, :], ALU.mult).then_inc(hidden_ready, 1)

            def tile(k, parity, first=False):
                gated(k)
                if not first:
                    dve.wait_ge(y_stored, 16 * k)
                rows_out(k + 1, 1 - parity)

            rows_out(0, 0)
            dve.wait_ge(up_mm, 1)
            tile(0, 0, first=True)
            with dve.Fori(1, TILES - 2, 2) as k:
                tile(k, 1)
                tile(k + 1, 0)
            tile(TILES - 2, 1)
            gated(TILES - 1)

            dve.wait_ge(y_loaded, 32)
            for b in range(B):
                tiles = slice(b * TT, (b + 1) * TT)
                own(dve.tensor_tensor(ya[:, tiles, :], ya[:, tiles, :], yb[:, tiles, :], ALU.add))
                own(dve.tensor_tensor(ya[:, tiles, :], ya[:, tiles, :],
                                      mods[:, b, 3, :].unsqueeze(1).to_broadcast([P, TT, D]), ALU.mult))
                dve.tensor_tensor(xs[:, tiles, :], xs[:, tiles, :], ya[:, tiles, :], ALU.add).then_inc(out_ready, 1)


def kernel(**inputs):
    import numpy as np
    import concourse.bacc as bacc
    from concourse.bass_utils import run_bass_kernel_spmd

    def laid(name, turn=False):
        a = np.asarray(inputs[name])
        return np.ascontiguousarray(a.T if turn else a)

    arrays = {
        "x": laid("L0_attn_x"),
        "wq": laid("L0_attn_Wq", True),
        "wk": laid("L0_attn_Wk", True),
        "wv": laid("L0_attn_Wv", True),
        "wo": laid("L0_attn_Wo", True),
        "gate_w": laid("L0_ffn_gate_w"),
        "w1": laid("L0_ffn_w1"),
        "w3": laid("L0_ffn_w3"),
        "w2": laid("L0_ffn_w2"),
        "c": laid("L0_c"),
        "wmod": laid("L0_wmod"),
    }
    nc = bacc.Bacc("TRN2", target_bir_lowering=False, num_devices=1)
    aps = [nc.dram_tensor(n, a.shape, mybir.dt.from_np(a.dtype), kind="ExternalInput").ap() for n, a in arrays.items()]
    out = nc.dram_tensor("out", [B, T, D], F32, kind="ExternalOutput").ap()
    build(nc, *aps, out)
    r = run_bass_kernel_spmd(nc, [arrays], core_ids=[0])
    return r.results[0]["out"]
```

```python
from contextlib import ExitStack

import concourse.bass as bass
from concourse import mybir

F32 = mybir.dt.float32
BF16 = mybir.dt.bfloat16
I32 = mybir.dt.int32
ALU = mybir.AluOpType
ACT = mybir.ActivationFunctionType
AX_X = mybir.AxisListType.X

P = 128
B, T, D = 4, 512, 256
NH, HD = 16, 16
E, F = 8, 512
N = B * T
DK = D // P
FK = F // P
TT = T // P
NT = N // P
EPS = 1e-5

HU = NH // 2
UNITS = B * 2
HG = 4
GROUPS = UNITS * HU // HG
NTERMS = 6
KS = NTERMS * HD
KB = KS + 3
Q_PART = (0, 0, 0, 1, 1, 2)
K_PART = (0, 1, 2, 0, 1, 0)
STACKS = 3

REGION = N + P
ROW = D + 2
DEST, WEIGHT = D, D + 1
NULL_ROW = E * REGION
HS_ROWS = E * REGION + P
TILES = 2 * N // P + E - 1
WCOLS = 2 * DK * F + FK * D
EARLY = 1
W1, W3, W2 = 0, DK * F, 2 * DK * F
NEG = -3.0e38
TWO_ONES = (1 << 23 | 0x3F80) / 2.0 ** 23


def scatters(b):
    return [("scatter", b, i, n) for i in range(TT) for n in range(2)]


WHEN = {
    "maxima": ((-0.197, 0.705), (-0.162, 0.648)),
    "max_rows": ((0.699, 0.763), (0.699, 0.79)),
    "max_split": ((0.563, 1.012), (0.438, 1.112)),
    "project": ((-0.13, 0.071), (-0.612, -0.502)),
    "split": ((-0.146, 0.441), (-0.162, 0.069)),
    "values": ((0.07, 0.345), (-0.626, -0.338)),
    "norm_stats": ((0.275, 1.275), (-0.356, -0.045)),
    "norm_rows": ((1.115, 1.298), (0.467, 0.8)),
    "h_cols": ((0.71, 0.71), (0.75, 0.799)),
    "back": ((0.227, 1.126), (-0.381, 0.619)),
    "gate": ((-0.37, -0.137), (-1.679, -0.679)),
    "choose": ((-0.163, -0.1), (0.527, 1.018)),
    "rank": ((-0.069, 0.03), (-0.475, -0.216)),
    "scatter": ((0.357, 0.635), (0.439, 1.021)),
    "value_sum": ((0.121, 0.172), (0.07, 0.089)),
    "last": ((0.48, 1.379), (1, 1)),
}


def attention_steps():
    timed = []

    def spread(s, where, steps):
        a, b = WHEN[where][s % 2] if isinstance(where, str) else where
        for j, step in enumerate(steps):
            timed.append((s + a + (b - a) * (j + 0.5) / len(steps), len(timed), step))

    for s in range(-2, UNITS + 1):
        if 0 <= s < UNITS:
            spread(s, (0, 1), [("score", 2 * s + n // SLOTS, n % SLOTS) for n in range(2 * SLOTS)])
            for g in range(2):
                for k in range(TT):
                    first, last = WHEN["value_sum"][g]
                    at = (g + (LAST_SLOT[k] + 1) / SLOTS) / 2 + first + (last - first) * k / (TT - 1)
                    spread(s, (at, at), [("value_sum", 2 * s + g, k)])
        u = s + 1
        if 0 <= u < UNITS:
            spread(s, "maxima", [("max_fill", u, n) for n in range(FILLS)])
            spread(s, "max_rows", [("max_rows", u)])
            spread(s, "max_split", [("max_split", u)])
        u = s + 2
        if u < UNITS:
            spread(s, "project", [("project", u, 0), ("project", u, 1)])
            spread(s, "split", [("split", u, 0), ("split", u, 1)])
            if u % 2 == 0:
                spread(s, "values", [("values", u // 2, i) for i in range(TT)])
        b = (s + 3) // 2
        if s % 2 and b < B:
            spread(s, "norm_stats", [("norm_stats", b)])
            spread(s, "norm_rows", [("norm_rows", b)])
            spread(s, "h_cols", [("h_cols", b, 0), ("h_cols", b, 1)])
        if s >= 2:
            b, half = (s - 2) // 2, s % 2
            first = b * TT + 2 * half
            last = s == UNITS
            tiles = range(b * TT, (b + 1) * TT) if last else (first, first + 1)
            kinds = ("z_rows", "z_cols", "out_rows", "norm2", "h2_cols", "router")
            lag = WHEN["last"][1][0 if last else 1]
            back = []
            for n in range(lag * (len(tiles) - 1) + len(kinds)):
                for j, t in enumerate(tiles):
                    if 0 <= n - lag * j < len(kinds):
                        back.append((kinds[n - lag * j], t))
            spread(s, WHEN["last"][0] if last else "back", back)
        if s >= 4 and s % 2 == 0:
            b = s // 2 - 2
            spread(s, "gate", [("gate", b)])
            spread(s, "choose", [("choose", b, n) for n in range(4)])
            spread(s, "rank", [("rank", b)])
            for half in range(2):
                spread(s, WHEN["scatter"][half], scatters(b)[half * TT:(half + 1) * TT])
        if s == -1:
            spread(s, (0.3, 0.3), [("constants", 1)])
        if s == UNITS - 2:
            spread(s, (0, 0), [("weights", e) for e in range(EARLY, 4)])
        if s == UNITS - 1:
            spread(s, (0, 0), [("weights", e) for e in range(4, 6)])
    b = B - 1
    return ([("norm_stats", 0), ("norm_rows", 0), ("h_cols", 0, 0), ("h_cols", 0, 1), ("constants", 0)] +
            [step for *_, step in sorted(timed)] + [("gate", b)] + [("choose", b, n) for n in range(4)] +
            [("rank", b)] + scatters(b) + [("weights", e) for e in (6, 7)])


FILLS = 2 + 4 + 8 + 8


def max_fill(n):
    if n < 2:
        return 0, 4 * n, 4
    if n < 6:
        return 1, 2 * (n - 2), 2
    i = 2 + (n - 6) // HU
    return i, (n - 6) % HU, 1


SLOTS = 4 + 4 + 2 + 1
ST = 3


LAST_SLOT = (3, 7, 9, 10)


def score_slot(n):
    if n < 8:
        return n // 4, n % 4, 1
    return ((2, 0, 2), (2, 2, 2), (3, 0, 4))[n - 8]


def build(nc, x, wq, wk, wv, wo, gate_w, w1, w3, w2, c, wmod, out):
    with ExitStack() as ctx:
        def sb(name, shape, dt=F32):
            return ctx.enter_context(nc.sbuf_tensor(name, shape, dt))

        def sem(name):
            return ctx.enter_context(nc.semaphore(name))

        split_dram = nc.dram_tensor("split_dram", [UNITS, 2, P, 3, T], BF16)
        max_dram = nc.dram_tensor("max_dram", [UNITS, HU, 3, T], BF16)
        mod_dram = nc.dram_tensor("mod_dram", [B, 6 * D], F32)
        routed_dram = nc.dram_tensor("routed_dram", [HS_ROWS, ROW], F32)
        expert_dram = nc.dram_tensor("expert_dram", [2 * N + P, D], F32)

        arena = sb("arena", [P, EARLY * WCOLS + 28160 + TT * D + 4 * T])
        weights = arena[:, 0:E * WCOLS].rearrange("p (e n) -> p e n", e=E)
        place = [EARLY * WCOLS]

        def scratch(cols):
            place[0] += cols
            return arena[:, place[0] - cols:place[0]]

        h_cols = [scratch(DK * T).rearrange("p (j t) -> p j t", j=DK) for _ in range(2)]
        parts = [scratch(3 * T // 2).bitcast(BF16).rearrange("p (a t) -> p a t", a=3) for _ in range(2)]
        rest = [scratch(T) for _ in range(2)]
        xn = scratch(TT * D).rearrange("p (i d) -> p i d", i=TT)
        v_rows = [scratch(TT * NH * 32).rearrange("p (i h d) -> p i h d", i=TT, h=NH)]
        stacks = [[scratch(HU * T // 2).bitcast(BF16).rearrange("p (h t) -> p h t", h=HU) for _ in range(2)]
                  for _ in range(STACKS)]
        turns = [(UNITS - STACKS + i) % STACKS for i in range(STACKS)]
        q_stack = [stacks[turns.index(i)][0] for i in range(STACKS)]
        k_stack = [stacks[turns.index(i)][1] for i in range(STACKS)]
        probs_all = scratch(HG * (512 + 384 + 256 + 128))
        v_rows.append(scratch(TT * NH * 32).rearrange("p (i h d) -> p i h d", i=TT, h=NH))
        z_all = [scratch(4 * T) for _ in range(2)]
        z_cols = [z.rearrange("p (g t) -> p g t", g=4) for z in z_all]
        tab_a = z_all[0][0:1, 0:TILES * E].rearrange("p (k e) -> p k e", e=E)
        tab_b = z_all[0][0:1, TILES * E:2 * TILES * E].rearrange("p (k e) -> p k e", e=E)
        probs, at = [], 0
        for k in range(TT):
            w = T - k * P
            probs.append(probs_all[:, at:at + HG * w].rearrange("p (h t) -> p h t", h=HG))
            at += HG * w
        wmod_sb = probs_all[:, 0:DK * 6 * D].rearrange("p (j n) -> p j n", j=DK)
        mod_rows = probs_all[0:B, DK * 6 * D:DK * 6 * D + 6 * D]
        place[0] = E * WCOLS
        xg = scratch(ROW)
        place[0] += ROW % 2
        xg_cols = scratch(D).rearrange("p (j t) -> p j t", j=DK)
        silu_sb = scratch(F)
        hidden = scratch(F)
        hidden_cols = scratch(F).rearrange("p (j t) -> p j t", j=FK)
        y_rows = scratch(D)
        tail = [scratch(2) for _ in range(4)]
        ya = arena[:, 0:NT * D].rearrange("p (t d) -> p t d", t=NT)
        yb = arena[:, NT * D:2 * NT * D].rearrange("p (t d) -> p t d", t=NT)

        xs = sb("xs", [P, NT, D])
        wqk_sb = sb("wqk_sb", [P, 2, DK, D])
        wv_sb = sb("wv_sb", [P, DK, D])
        wo_sb = sb("wo_sb", [P, DK, D])
        wog = sb("wog", [P, DK, D])
        gate_sb = sb("gate_sb", [P, DK, E])
        mods = sb("mods", [P, B, 4, D])
        mod_cols = sb("mod_cols", [P, 4, B])
        h2x = sb("h2x", [P, TT, 2, ROW])
        h2_cols = sb("h2_cols", [P, DK, P])
        zn = sb("zn", [P, NH, HD])
        zn_cols = sb("zn_cols", [P, DK, P])
        z_recip = sb("z_recip", [P, NH])
        ident = sb("ident", [P, P])
        identb = sb("identb", [P, P], BF16)
        causal = sb("causal", [P, P], BF16)
        earlier = sb("earlier", [P, P], BF16)
        onesb = sb("onesb", [P, P], BF16)
        c_sb = sb("c_sb", [B, D])
        c_cols = sb("c_cols", [P, DK, B])
        c_exp = sb("c_exp", [P, DK, B])
        c_silu = sb("c_silu", [P, DK, B])
        gtmp = sb("gtmp", [B, 2, D])
        stats = sb("stats", [P, TT, 6])
        moments = sb("moments", [P, TT, 2])
        rstd = sb("rstd", [P, TT])
        stats2 = sb("stats2", [P, 6])
        moments2 = sb("moments2", [P, 2, 2])
        rstd2 = sb("rstd2", [P, 2])
        minus_half = sb("minus_half", [P, TT])
        row_max = sb("row_max", [P, 2, TT, HU])
        max_parts = sb("max_parts", [HU, 3, T], BF16)
        max_rest = sb("max_rest", [HU, T])
        logits = sb("logits", [P, TT, E])
        gate_exp = sb("gate_exp", [P, TT, E])
        gate_p = sb("gate_p", [P, TT, E])
        gate_t = sb("gate_t", [P, TT, E])
        hot = sb("hot", [P, 2, TT, E])
        gate_s = sb("gate_s", [P, 4, TT])
        top_w = sb("top_w", [P, 2, TT])
        chosen = sb("chosen", [P, NT, E], BF16)
        before = sb("before", [P, NT + 1, E], BF16)
        rank_pos = sb("rank_pos", [P, TT, E])
        pos_f = sb("pos_f", [P, 2, TT])
        pos_i = sb("pos_i", [P, 2, TT], I32)
        rev_e = sb("rev_e", [P, E])
        base_e = sb("base_e", [P, E])
        part_base = sb("part_base", [P, E])
        dest = sb("dest", [P, 2, NT], I32)
        null_rows = sb("null_rows", [P, ROW])
        fill_f = sb("fill_f", [P, E])
        fill_i = sb("fill_i", [P, E], I32)
        count_f = sb("count_f", [1, E])
        count_i = sb("count_i", [1, E], I32)
        ntile = sb("ntile", [1, E])
        ends = sb("ends", [1, 4, E])
        tile_no = sb("tile_no", [1, TILES])
        tab_v = sb("tab_v", [1, 6, TILES])
        table = sb("table", [1, 2, TILES], I32)

        st = [ctx.enter_context(nc.psum_tensor(f"st{i}", [P, 512], F32)) for i in range(ST)]
        mx = [ctx.enter_context(nc.psum_tensor(f"mx{i}", [P, 512], F32)) for i in range(2)]
        pv = ctx.enter_context(nc.psum_tensor("pv", [P, 512], F32))
        misc2 = [ctx.enter_context(nc.psum_tensor(f"misc{i}", [P, 512], F32)) for i in range(2)]

        x_loaded = [sem(f"x_loaded{b}") for b in range(B)]
        small_loaded = sem("small_loaded")
        wmod_loaded = [sem(f"wmod_loaded{n}") for n in range(3)]
        attn_w_loaded = sem("attn_w_loaded")
        first_w_loaded = sem("first_w_loaded")
        last_w_loaded = sem("last_w_loaded")
        pool_const = sem("pool_const")
        ones_made = sem("ones_made")
        mod_ready = sem("mod_ready")
        mod_stored = sem("mod_stored")
        mods_loaded = sem("mods_loaded")
        c_step = sem("c_step")
        c_ready = sem("c_ready")
        setup_mm = sem("setup_mm")
        setup_dve = sem("setup_dve")
        wog_ready = sem("wog_ready")
        stats_ready = sem("stats_ready")
        rstd_ready = sem("rstd_ready")
        xn_ready = sem("xn_ready")
        misc_filled = sem("misc_filled")
        act_evac = sem("act_evac")
        dve_evac = sem("dve_evac")
        high_ready = sem("high_ready")
        mid_ready = sem("mid_ready")
        low_ready = sem("low_ready")
        parts_stored = [sem(f"parts_stored{w}") for w in range(2)]
        stack_loaded = [sem(f"stack_loaded{i}") for i in range(STACKS)]
        mx_filled = sem("mx_filled")
        mx_drained = sem("mx_drained")
        mhigh_ready = sem("mhigh_ready")
        mmid_ready = sem("mmid_ready")
        mlow_ready = sem("mlow_ready")
        max_stored = sem("max_stored")
        max_loaded = [sem(f"max_loaded{i}") for i in range(STACKS)]
        st_filled = sem("st_filled")
        exp_done = sem("exp_done")
        pv_done = sem("pv_done")
        z_copied = sem("z_copied")
        stats2_ready = sem("stats2_ready")
        rstd2_ready = sem("rstd2_ready")
        xn2_ready = sem("xn2_ready")
        h2_ready = sem("h2_ready")
        h2_copied = sem("h2_copied")
        shifted = sem("shifted")
        gate_exped = sem("gate_exped")
        chosen_ready = sem("chosen_ready")
        routed = sem("routed")
        scattered = [sem(f"scattered{i}") for i in range(TT)]
        filled = sem("filled")
        fill_ready = sem("fill_ready")
        table_ready = sem("table_ready")
        null_stored = sem("null_stored")
        vec_step = sem("vec_step")
        pool_step = sem("pool_step")
        xg_loaded = sem("xg_loaded")
        xg_turned = sem("xg_turned")
        cols_copied = sem("cols_copied")
        tail_copied = sem("tail_copied")
        gate_mm = sem("gate_mm")
        up_mm = sem("up_mm")
        silu_done = sem("silu_done")
        hidden_ready = sem("hidden_ready")
        hidden_turned = sem("hidden_turned")
        hidden_copied = sem("hidden_copied")
        y_mm = sem("y_mm")
        y_copied = sem("y_copied")
        y_stored = sem("y_stored")
        store_turn = sem("store_turn")
        y_loaded = sem("y_loaded")
        out_ready = sem("out_ready")
        out_stored = sem("out_stored")

        STEPS = attention_steps()
        IDENT_MADE, CAUSAL_MADE, V0_MADE, NULL_MADE, V1_MADE, CONSTS = 2, 4, 5, 6, 7, 15
        ON_ACT = ("h_cols", "values", "z_cols", "h2_cols", "router")
        ON_DVE = ("project", "max_rows", "z_rows", "out_rows", "rank")
        use, evacs = {}, {"act": 0, "dve": 0}
        for key in STEPS:
            if key[0] in ON_ACT + ON_DVE:
                who = "act" if key[0] in ON_ACT else "dve"
                evacs[who] += 1
                use[key] = (len(use), who, evacs[who])
        use_order = sorted(use, key=lambda k: use[k][0])

        def bank_of(key):
            return misc2[use[key][0] % 2] if key in use else None

        def wait_filled(eng, key):
            eng.wait_ge(misc_filled, use[key][0] + 1)

        def wait_evacuated(eng, key):
            _, who, count = use[key]
            eng.wait_ge(act_evac if who == "act" else dve_evac, count)

        def stack_turn(u):
            return u // STACKS + 1

        block = ctx.enter_context(nc.Block())

        @block.sync
        def _(sp):
            sp.dma_start(c_sb[:, :], c).then_inc(small_loaded, 16)
            xv = x.rearrange("b (i p) d -> b p i d", p=P)
            sp.dma_start(xs[:, 0:TT, :], xv[0]).then_inc(x_loaded[0], 16)
            wmod_cols = wmod.rearrange("(j p) n -> p j n", p=P)
            sp.dma_start(wmod_sb[:, :, 0:512], wmod_cols[:, :, 0:512]).then_inc(wmod_loaded[0], 16)
            for n, w in enumerate((wq, wk)):
                sp.dma_start(wqk_sb[:, n], w.rearrange("(j p) n -> p j n", p=P)).then_inc(attn_w_loaded, 16)
            sp.dma_start(wv_sb[:, :, :], wv.rearrange("(j p) n -> p j n", p=P)).then_inc(attn_w_loaded, 16)
            sp.dma_start(wo_sb[:, :, :], wo.rearrange("(j p) n -> p j n", p=P)).then_inc(attn_w_loaded, 16)
            sp.dma_start(gate_sb[:, :, :], gate_w.rearrange("(j p) n -> p j n", p=P)).then_inc(attn_w_loaded, 16)
            for n in range(1, 3):
                sp.dma_start(wmod_sb[:, :, n * 512:(n + 1) * 512], wmod_cols[:, :, n * 512:(n + 1) * 512]).then_inc(wmod_loaded[n], 16)
            for b in range(1, B):
                sp.dma_start(xs[:, b * TT:(b + 1) * TT, :], xv[b]).then_inc(x_loaded[b], 16)
            def load_weights(e, done):
                sp.dma_start(weights[:, e, W1:W3].rearrange("p (j f) -> p j f", j=DK),
                             w1[e].rearrange("(j p) f -> p j f", p=P)).then_inc(done, 16)
                sp.dma_start(weights[:, e, W3:W2].rearrange("p (j f) -> p j f", j=DK),
                             w3[e].rearrange("(j p) f -> p j f", p=P)).then_inc(done, 16)
                sp.dma_start(weights[:, e, W2:WCOLS].rearrange("p (j d) -> p j d", j=FK),
                             w2[e].rearrange("(j p) d -> p j d", p=P)).then_inc(done, 16)

            early = 0
            for key in STEPS:
                if key == ("constants", 1):
                    sp.wait_ge(pool_const, NULL_MADE)
                    sp.dma_start(routed_dram[NULL_ROW:NULL_ROW + P, :], null_rows[:, :]).then_inc(null_stored, 16)
                if key[0] == "weights":
                    e = key[1]
                    if e < 4:
                        sp.wait_ge(pv_done, 4 * (GROUPS - 4))
                    elif e < 6:
                        sp.wait_ge(pv_done, 4 * (GROUPS - 2))
                    else:
                        sp.wait_ge(pv_done, 4 * GROUPS)
                    load_weights(e, last_w_loaded)
                if key[0] == "split":
                    _, u, w = key
                    sp.wait_ge(low_ready, 2 * u + w + 1)
                    sp.dma_start(split_dram[u, w], parts[w]).then_inc(parts_stored[w], 16)
                    sp.wait_ge(parts_stored[w], 16 * (u + 1))
                    if u >= STACKS:
                        sp.wait_ge(st_filled, 2 * SLOTS * (u - STACKS + 1))
                    stack = (q_stack, k_stack)[w][u % STACKS]
                    for g in range(NTERMS):
                        part = (Q_PART, K_PART)[w][g]
                        src = split_dram[u, w, :, part, :].rearrange("(h d) t -> d h t", d=HD)
                        sp.dma_start(stack[g * HD:(g + 1) * HD, :, :], src).then_inc(stack_loaded[u % STACKS], 16)
                    if u == 0 and w == 1:
                        sp.wait_ge(mod_ready, 1)
                        sp.dma_start(mod_dram[:, :], mod_rows).then_inc(mod_stored, 16)
                        sp.wait_ge(mod_stored, 16)
                        sp.dma_start(mods[:, :, :, :].rearrange("p b m d -> p b (m d)"),
                                     mod_dram[:, 2 * D:6 * D].partition_broadcast(P)).then_inc(mods_loaded, 16)
                    if early < EARLY and u == 1 and w == 1:
                        load_weights(early, first_w_loaded)
                        early += 1
                if key[0] == "max_split":
                    u = key[1]
                    sp.wait_ge(mlow_ready, u + 1)
                    sp.dma_start(max_dram[u], max_parts[:, :, :]).then_inc(max_stored, 16)
                    sp.wait_ge(max_stored, 16 * (u + 1))
                    sp.dma_start(q_stack[u % STACKS][KS:KB, :, :],
                                 max_dram[u].rearrange("h a t -> a h t")).then_inc(max_loaded[u % STACKS], 16)
            sp.wait_ge(table_ready, 1)
            for i in range(TT):
                sp.wait_ge(scattered[i], 16 * 2 * B)
            sp.wait_ge(filled, 16 * E)
            sp.wait_ge(null_stored, 16)

            def load_rows(k, first=False):
                row = sp.value_load(table[0:1, 1, bass.ds(k, 1)], min_val=0, max_val=NULL_ROW)
                if not first:
                    sp.wait_ge(tail_copied, k)
                sp.dma_start(xg, routed_dram[bass.ds(row, P), :]).then_inc(xg_loaded, 16)

            load_rows(0, first=True)
            with sp.Fori(1, TILES) as k:
                load_rows(k)
            sp.wait_ge(y_stored, 16 * TILES)
            sp.dma_start(ya, expert_dram[0:N, :].rearrange("(t p) d -> p t d", p=P)).then_inc(y_loaded, 16)
            sp.dma_start(yb, expert_dram[N:2 * N, :].rearrange("(t p) d -> p t d", p=P)).then_inc(y_loaded, 16)
            outv = out.rearrange("b (i p) d -> b p i d", p=P)
            for b in range(B):
                sp.wait_ge(out_ready, b + 1)
                sp.dma_start(outv[b], xs[:, b * TT:(b + 1) * TT, :]).then_inc(out_stored, 16)
            sp.wait_ge(out_stored, 16 * B)

        @block.gpsimd
        def _(pool):
            steps = [0]

            def own(ins):
                steps[0] += 1
                ins.then_inc(pool_step, 1)
                pool.wait_ge(pool_step, steps[0])

            consts = [0]

            def const(ins):
                consts[0] += 1
                ins.then_inc(pool_const, 1)
                pool.wait_ge(pool_const, consts[0])

            def made(count):
                assert consts[0] == count

            const(pool.memset(minus_half[:, :], -0.5))
            own(pool.memset(ident[:, :], 0.0))
            const(pool.affine_select(out=ident[:, :], in_=ident[:, :], compare_op=ALU.not_equal, fill=1.0, base=0,
                                     pattern=[[-1, P]], channel_multiplier=1))
            made(IDENT_MADE)
            const(pool.tensor_copy(identb[:, :], ident[:, :]))

            def first_constants():
                own(pool.memset(causal[:, :], 0.0))
                const(pool.affine_select(out=causal[:, :], in_=causal[:, :], compare_op=ALU.is_ge, fill=NEG, base=0,
                                         pattern=[[-1, P]], channel_multiplier=1))
                made(CAUSAL_MADE)

            def early_constants():
                own(pool.memset(v_rows[0], 0.0))
                const(pool.memset(v_rows[0][:, :, :, HD:HD + 1], 1.0))
                made(V0_MADE)
                own(pool.memset(null_rows[:, :], 0.0))
                const(pool.iota(null_rows[:, DEST:DEST + 1].bitcast(I32), pattern=[[0, 1]], base=2 * N,
                                channel_multiplier=1))
                made(NULL_MADE)

            def late_constants():
                own(pool.memset(v_rows[1], 0.0))
                const(pool.memset(v_rows[1][:, :, :, HD:HD + 1], 1.0))
                made(V1_MADE)
                own(pool.memset(earlier[:, :], 1.0))
                const(pool.affine_select(out=earlier[:, :], in_=earlier[:, :], compare_op=ALU.is_gt, fill=0.0, base=0,
                                         pattern=[[1, P]], channel_multiplier=-1))
                const(pool.memset(onesb[:, :], 1.0))
                const(pool.iota(rev_e[:, :], pattern=[[-1, E]], base=E, channel_multiplier=0,
                                allow_small_or_imprecise_dtypes=True))
                const(pool.iota(base_e[:, :], pattern=[[REGION, E]], base=0, channel_multiplier=0,
                                allow_small_or_imprecise_dtypes=True))
                const(pool.iota(part_base[:, :], pattern=[[REGION, E]], base=0, channel_multiplier=1,
                                allow_small_or_imprecise_dtypes=True))
                const(pool.iota(dest[:, :, :], pattern=[[N, 2], [P, NT]], base=0, channel_multiplier=1))
                const(pool.iota(tile_no[:, :], pattern=[[1, TILES]], base=0, channel_multiplier=0,
                                allow_small_or_imprecise_dtypes=True))
                const(pool.memset(before[:, 0, :], 0.0))
                made(CONSTS)

            for key in STEPS:
                kind = key[0]
                if kind == "norm_stats":
                    b = key[1]
                    pool.wait_ge(stats_ready, b + 1)
                    own(pool.tensor_scalar(rstd[:, :], moments[:, :, 1], EPS, None, ALU.add))
                    pool.tensor_tensor(rstd[:, :], rstd[:, :], minus_half[:, :], ALU.pow).then_inc(rstd_ready, 1)
                    if b == 0:
                        first_constants()
                elif kind == "split":
                    _, u, w = key
                    n = 2 * u + w
                    pool.wait_ge(mid_ready, n + 1)
                    pool.tensor_tensor(parts[w][:, 2, :], rest[w], parts[w][:, 1, :], ALU.subtract).then_inc(low_ready, 1)
                elif kind == "constants":
                    (early_constants, late_constants)[key[1]]()
                elif kind == "max_split":
                    u = key[1]
                    pool.wait_ge(mmid_ready, u + 1)
                    pool.tensor_tensor(max_parts[:, 2, :], max_rest[:, :], max_parts[:, 1, :],
                                       ALU.subtract).then_inc(mlow_ready, 1)
                elif kind == "z_rows" and key[1] % TT == 0:
                    b = key[1] // TT
                    if b == 0:
                        pool.wait_ge(mods_loaded, 16)
                        pool.wait_ge(attn_w_loaded, 80)
                    else:
                        wait_filled(pool, ("out_rows", b * TT - 1))
                    pool.tensor_tensor(wog[:, :, :], wo_sb[:, :, :],
                                       mods[:, b, 0, :].unsqueeze(1).to_broadcast([P, DK, D]), ALU.mult).then_inc(wog_ready, 1)
                elif kind == "out_rows":
                    t = key[1]
                    pool.wait_ge(stats2_ready, t + 1)
                    own(pool.tensor_scalar(rstd2[:, t % 2:t % 2 + 1], moments2[:, t % 2, 1:2], EPS, None, ALU.add))
                    pool.tensor_tensor(rstd2[:, t % 2:t % 2 + 1], rstd2[:, t % 2:t % 2 + 1], minus_half[:, 0:1],
                                       ALU.pow).then_inc(rstd2_ready, 1)
                elif kind == "norm2":
                    t = key[1]
                    b, i = t // TT, t % TT
                    row = h2x[:, i, 0, 0:D]
                    pool.wait_ge(xn2_ready, t + 1)
                    own(pool.tensor_tensor(row, row, mods[:, b, 2, :], ALU.mult))
                    pool.tensor_tensor(row, row, mods[:, b, 1, :], ALU.add).then_inc(h2_ready, 1)
                elif kind == "scatter":
                    _, b, i, n = key
                    pool.wait_ge(routed, b + 1)
                    pool.wait_ge(h2_copied, (b + 1) * TT)
                    pool.indirect_dma_start(
                        out=routed_dram[:, :], out_offset=bass.IndirectOffsetOnAxis(ap=pos_i[:, n, i:i + 1], axis=0),
                        in_=h2x[:, i, n, :], in_offset=None).then_inc(scattered[i], 16)
            pool.wait_ge(fill_ready, 1)
            for e in range(E):
                pool.indirect_dma_start(
                    out=routed_dram[:, :], out_offset=bass.IndirectOffsetOnAxis(ap=fill_i[:, e:e + 1], axis=0),
                    in_=null_rows[:, :], in_offset=None).then_inc(filled, 16)

            def store_rows(k, turn):
                pool.wait_ge(y_copied, k + 1)
                pool.sem_inc(store_turn, 1)
                pool.indirect_dma_start(
                    out=expert_dram[:, :],
                    out_offset=bass.IndirectOffsetOnAxis(ap=tail[turn][:, 0:1].bitcast(I32), axis=0),
                    in_=y_rows, in_offset=None).then_inc(y_stored, 16)

            store_rows(0, 0)
            with pool.Fori(1, TILES - 2, 4) as k:
                for n in range(4):
                    store_rows(k + n, (1 + n) % 4)
            for k in range(TILES - 2, TILES):
                store_rows(k, k % 4)

        @block.scalar
        def _(act):
            act.wait_ge(setup_dve, 1)
            act.activation(c_exp[:, :, :], c_cols[:, :, :], ACT.Exp, scale=-1.0).then_inc(c_step, 1)
            for key in STEPS:
                kind, misc = key[0], bank_of(key)
                if kind == "h_cols":
                    _, b, j = key
                    act.wait_ge(setup_dve, 4)
                    wait_filled(act, key)
                    act.activation(h_cols[b % 2][:, j, :], misc[:, :], ACT.Identity,
                                   bias=mod_cols[:, j, b:b + 1], scale=mod_cols[:, 2 + j, b:b + 1]).then_inc(act_evac, 1)
                elif kind == "values":
                    _, b, i = key
                    act.wait_ge(pool_const, V1_MADE if b else V0_MADE)
                    wait_filled(act, key)
                    act.activation(v_rows[b % 2][:, i, :, 0:HD], misc[:, 0:D].rearrange("p (h d) -> p h d", h=NH),
                                   ACT.Copy).then_inc(act_evac, 1)
                elif kind == "project":
                    _, u, w = key
                    wait_filled(act, key)
                    if u >= 1:
                        act.wait_ge(parts_stored[w], 16 * u)
                    act.activation(parts[w][:, 0, :], misc[:, :], ACT.Copy,
                                   scale=(HD ** -0.5, 1.0)[w]).then_inc(high_ready, 1)
                elif kind == "split":
                    _, u, w = key
                    wait_evacuated(act, ("project", u, w))
                    act.activation(parts[w][:, 1, :], rest[w], ACT.Copy).then_inc(mid_ready, 1)
                elif kind == "max_rows":
                    u = key[1]
                    wait_filled(act, key)
                    if u >= 1:
                        act.wait_ge(max_stored, 16 * u)
                    act.activation(max_parts[:, 0, :], misc[0:HU, :], ACT.Copy, scale=-1.0).then_inc(mhigh_ready, 1)
                elif kind == "max_split":
                    u = key[1]
                    wait_evacuated(act, ("max_rows", u))
                    act.activation(max_parts[:, 1, :], max_rest[:, :], ACT.Copy).then_inc(mmid_ready, 1)
                elif kind == "score":
                    _, g, n = key
                    k, h0, nh = score_slot(n)
                    w = T - k * P
                    s = SLOTS * g + n
                    if s == 0:
                        act.wait_ge(mod_stored, 16)
                    if g >= 1:
                        act.wait_ge(pv_done, 4 * (g - 1) + k + 1)
                    act.wait_ge(st_filled, s + 1)
                    src = st[s % ST][:, 0:nh * w].rearrange("p (h t) -> p h t", h=nh)
                    act.activation(probs[k][:, h0:h0 + nh, :], src, ACT.Exp).then_inc(exp_done, 1)
                elif kind == "value_sum":
                    _, g, k = key
                    if k == TT - 1:
                        act.wait_ge(pv_done, 4 * (g + 1))
                        if g >= 8:
                            wait_filled(act, ("z_rows", (g // 4 - 1) * TT - 1))
                        act.activation(z_cols[g // 4 % 2][:, g % 4, :], pv[:, :], ACT.Copy).then_inc(z_copied, 1)
                elif kind == "z_cols":
                    wait_filled(act, key)
                    act.activation(zn_cols[:, :, :].rearrange("p j t -> p (j t)"), misc[:, 0:D], ACT.Copy).then_inc(act_evac, 1)
                elif kind == "h2_cols":
                    t = key[1]
                    wait_filled(act, key)
                    act.activation(h2_cols[:, :, :].rearrange("p j t -> p (j t)"), misc[:, 0:D], ACT.Copy).then_inc(act_evac, 1)
                    act.activation(h2x[:, t % TT, 1, 0:D], h2x[:, t % TT, 0, 0:D], ACT.Copy).then_inc(h2_copied, 1)
                elif kind == "router":
                    t = key[1]
                    wait_filled(act, key)
                    if t >= TT:
                        act.wait_ge(shifted, t // TT)
                    act.activation(logits[:, t % TT, :], misc[:, 0:E], ACT.Copy).then_inc(act_evac, 1)
                elif kind == "gate":
                    b = key[1]
                    act.wait_ge(shifted, b + 1)
                    act.activation(gate_exp[:, :, :], gate_t[:, :, :], ACT.Exp).then_inc(gate_exped, 1)

            def silu(k):
                act.wait_ge(gate_mm, k + 1)
                act.activation(silu_sb, mx[0][:, :], ACT.Silu).then_inc(silu_done, 1)

            def hidden_out(k):
                act.wait_ge(hidden_turned, k + 1)
                act.activation(hidden_cols.rearrange("p j t -> p (j t)"), pv[:, :], ACT.Copy).then_inc(hidden_copied, 1)

            def y_out(k, turn, first=False):
                if not first:
                    act.wait_ge(y_stored, 16 * k)
                act.wait_ge(y_mm, k + 1)
                act.activation(y_rows, st[0][:, 0:D], ACT.Copy, scale=tail[turn][:, 1:2]).then_inc(y_copied, 1)

            silu(0)

            def tile(k, turn, first=False):
                hidden_out(k - 1)
                act.wait_ge(hidden_ready, k)
                silu(k)
                act.wait_ge(tail_copied, k)
                y_out(k - 1, (turn + 3) % 4, first)

            tile(1, 1, first=True)
            with act.Fori(2, TILES - 1, 4) as k:
                for n in range(4):
                    tile(k + n, (2 + n) % 4)
            tile(TILES - 1, (TILES - 1) % 4)
            hidden_out(TILES - 1)
            act.wait_ge(tail_copied, TILES)
            y_out(TILES - 1, (TILES - 1) % 4)

        @block.tensor
        def _(pe):
            pe.wait_ge(small_loaded, 16)
            pe.wait_ge(pool_const, IDENT_MADE)
            for j in range(DK):
                ins = pe.transpose(misc2[0][:, j * B:(j + 1) * B], c_sb[:, j * P:(j + 1) * P], ident[0:B, 0:B])
            ins.then_inc(setup_mm, 1)
            pe.wait_ge(c_ready, 1)
            for n, bank in enumerate((mx[0][0:B, :], mx[1][0:B, :], pv[0:B, :])):
                pe.wait_ge(wmod_loaded[n], 16)
                for j in range(DK):
                    ins = pe.matmul(bank, c_silu[:, j, :], wmod_sb[:, j, n * 512:(n + 1) * 512],
                                    start=(j == 0), stop=(j == DK - 1))
                ins.then_inc(setup_mm, 1)
                if n == 0:
                    pe.wait_ge(setup_dve, 3)
                    for m in range(4):
                        ins = pe.transpose(misc2[0][:, m * B:(m + 1) * B], mod_rows[:, m * P:(m + 1) * P], ident[0:B, 0:B])
                    ins.then_inc(setup_mm, 1)
            pe.wait_ge(setup_dve, 4)
            pe.wait_ge(attn_w_loaded, 80)

            for key in STEPS:
                kind = key[0]
                misc = bank_of(key)
                if key in use and use[key][0] >= 2:
                    wait_evacuated(pe, use_order[use[key][0] - 2])
                if kind == "h_cols":
                    _, b, j = key
                    pe.wait_ge(xn_ready, TT * (b + 1))
                    for i in range(TT):
                        ins = pe.transpose(misc[:, i * P:(i + 1) * P], xn[:, i, j * P:(j + 1) * P], ident[:, :])
                    ins.then_inc(misc_filled, 1)
                elif kind == "values":
                    _, b, i = key
                    wait_evacuated(pe, ("h_cols", b, 1))
                    for j in range(DK):
                        ins = pe.matmul(misc[:, 0:D], h_cols[b % 2][:, j, i * P:(i + 1) * P], wv_sb[:, j, :],
                                        start=(j == 0), stop=(j == DK - 1))
                    ins.then_inc(misc_filled, 1)
                elif kind == "project":
                    _, u, w = key
                    b, half = u // 2, u % 2
                    wait_evacuated(pe, ("h_cols", b, 1))
                    for j in range(DK):
                        ins = pe.matmul(misc[:, :], wqk_sb[:, w, j, half * P:(half + 1) * P], h_cols[b % 2][:, j, :],
                                        start=(j == 0), stop=(j == DK - 1))
                    ins.then_inc(misc_filled, 1)
                elif kind == "max_fill":
                    _, u, n = key
                    i, h0, nh = max_fill(n)
                    w = (i + 1) * P
                    f = FILLS * u + n
                    if n == 0 and u == 0:
                        pe.wait_ge(pool_const, CAUSAL_MADE)
                        pe.wait_ge(mod_ready, 1)
                    if n == 0:
                        pe.wait_ge(stack_loaded[u % STACKS], 16 * 2 * NTERMS * stack_turn(u))
                    if f >= 2:
                        pe.wait_ge(mx_drained, f - 1)
                    bank = mx[f % 2]
                    qs, ks = q_stack[u % STACKS], k_stack[u % STACKS]
                    for a in range(nh):
                        pe.matmul(bank[:, a * w:(a + 1) * w], qs[0:KS, h0 + a, i * P:(i + 1) * P], ks[0:KS, h0 + a, 0:w],
                                  start=(a == 0), stop=False, skip_group_check=True)
                    diag = bank[:, 0:nh * w].rearrange("p (h s) -> p h s", h=nh)[:, :, i * P:(i + 1) * P]
                    pe.matmul(diag, identb[:, :], causal[:, :].unsqueeze(1).to_broadcast([P, nh, P]),
                              start=False, stop=True, skip_group_check=True).then_inc(mx_filled, 1)
                elif kind == "max_rows":
                    u = key[1]
                    pe.wait_ge(mx_drained, FILLS * (u + 1))
                    for i in range(TT):
                        ins = pe.transpose(misc[0:HU, i * P:(i + 1) * P], row_max[:, u % 2, i, :], ident[:, :])
                    ins.then_inc(misc_filled, 1)
                elif kind == "score":
                    _, g, n = key
                    u = g // 2
                    k, h0, nh = score_slot(n)
                    w = T - k * P
                    s = SLOTS * g + n
                    if s >= ST:
                        pe.wait_ge(exp_done, s - ST + 1)
                    if s == 0:
                        pe.wait_ge(ones_made, STACKS)
                    if n == 0 and g % 2 == 0:
                        pe.wait_ge(max_loaded[u % STACKS], 16 * stack_turn(u))
                    qs, ks = q_stack[u % STACKS], k_stack[u % STACKS]
                    for a in range(nh):
                        h = (g % 2) * HG + h0 + a
                        pe.matmul(st[s % ST][:, a * w:(a + 1) * w], ks[0:KB, h, k * P:(k + 1) * P],
                                  qs[0:KB, h, k * P:T], start=(a == 0), stop=False, skip_group_check=True)
                    diag = st[s % ST][:, 0:nh * w].rearrange("p (h t) -> p h t", h=nh)[:, :, 0:P]
                    pe.matmul(diag, causal[:, :], identb[:, :].unsqueeze(1).to_broadcast([P, nh, P]),
                              start=False, stop=True, skip_group_check=True).then_inc(st_filled, 1)
                elif kind == "value_sum":
                    _, g, k = key
                    b = g // 4
                    pe.wait_ge(exp_done, SLOTS * g + LAST_SLOT[k] + 1)
                    if k == 0:
                        wait_evacuated(pe, ("values", b, TT - 1))
                        if g >= 1:
                            pe.wait_ge(z_copied, g)
                    for a in range(HG):
                        h = (g % 4) * HG + a
                        ins = pe.matmul(pv[32 * a:32 * a + 32, k * P:T], v_rows[b % 2][:, k, h, :], probs[k][:, a, :],
                                        start=(k == 0), stop=(k == TT - 1), skip_group_check=True)
                    ins.then_inc(pv_done, 1)
                elif kind == "z_rows":
                    t = key[1]
                    b, i = t // TT, t % TT
                    pe.wait_ge(z_copied, 4 * (b + 1))
                    for g in range(4):
                        ins = pe.transpose(misc[:, g * P:(g + 1) * P], z_cols[b % 2][:, g, i * P:(i + 1) * P], ident[:, :])
                    ins.then_inc(misc_filled, 1)
                elif kind == "z_cols":
                    t = key[1]
                    wait_evacuated(pe, ("z_rows", t))
                    for j in range(DK):
                        ins = pe.transpose(misc[:, j * P:(j + 1) * P],
                                           zn[:, j * HU:(j + 1) * HU, :].rearrange("p h d -> p (h d)"), ident[:, :])
                    ins.then_inc(misc_filled, 1)
                elif kind == "out_rows":
                    t = key[1]
                    wait_evacuated(pe, ("z_cols", t))
                    pe.wait_ge(wog_ready, t // TT + 1)
                    for j in range(DK):
                        ins = pe.matmul(misc[:, 0:D], zn_cols[:, j, :], wog[:, j, :], start=(j == 0), stop=(j == DK - 1))
                    ins.then_inc(misc_filled, 1)
                elif kind == "h2_cols":
                    t = key[1]
                    pe.wait_ge(h2_ready, t + 1)
                    for j in range(DK):
                        ins = pe.transpose(misc[:, j * P:(j + 1) * P], h2x[:, t % TT, 0, j * P:(j + 1) * P], ident[:, :])
                    ins.then_inc(misc_filled, 1)
                elif kind == "router":
                    t = key[1]
                    wait_evacuated(pe, ("h2_cols", t))
                    for j in range(DK):
                        ins = pe.matmul(misc[:, 0:E], h2_cols[:, j, :], gate_sb[:, j, :], start=(j == 0), stop=(j == DK - 1))
                    ins.then_inc(misc_filled, 1)
                elif kind == "rank":
                    b = key[1]
                    pe.wait_ge(chosen_ready, b + 1)
                    if b == 0:
                        pe.wait_ge(pool_const, CONSTS)
                    for i in range(TT):
                        t = b * TT + i
                        pe.matmul(misc[:, i * E:(i + 1) * E], earlier[:, :], chosen[:, t, :],
                                  start=(i == 0), stop=False, skip_group_check=True)
                        ins = pe.matmul(misc[:, i * E:(i + 1) * E], onesb[:, :], before[:, t, :],
                                        start=False, stop=(i == TT - 1), skip_group_check=True)
                    ins.then_inc(misc_filled, 1)
            wait_evacuated(pe, use_order[-1])
            wait_evacuated(pe, use_order[-2])
            pe.matmul(misc2[0][:, 0:E], onesb[:, :], before[:, NT, :], start=True, stop=True).then_inc(setup_mm, 1)

            pe.wait_ge(first_w_loaded, 16 * 3 * EARLY)
            pe.wait_ge(last_w_loaded, 16 * 3 * (E - EARLY))
            pe.wait_ge(table_ready, 1)
            pe.wait_ge(exp_done, SLOTS * GROUPS)
            pe.wait_ge(z_copied, GROUPS)
            pe.wait_ge(mx_drained, FILLS * UNITS)

            def expert_of(k):
                return pe.value_load(table[0:1, 0, bass.ds(k, 1)], min_val=0, max_val=E - 1)

            def turn_rows(k):
                pe.wait_ge(xg_loaded, 16 * (k + 1))
                for j in range(DK):
                    ins = pe.transpose(misc2[0][:, j * P:(j + 1) * P], xg[:, j * P:(j + 1) * P], ident[:, :])
                ins.then_inc(xg_turned, 1)

            def up(k, e, col, bank, done):
                for j in range(DK):
                    w = arena[:, bass.ds(e * WCOLS + (col + j * F), F)]
                    ins = pe.matmul(bank[:, :], xg_cols[:, j, :], w, start=(j == 0), stop=(j == DK - 1))
                ins.then_inc(done, 1)

            def turn_hidden(k):
                pe.wait_ge(hidden_ready, k + 1)
                for j in range(FK):
                    ins = pe.transpose(pv[:, j * P:(j + 1) * P], hidden[:, j * P:(j + 1) * P], ident[:, :])
                ins.then_inc(hidden_turned, 1)

            def down(k, e, first=False):
                pe.wait_ge(hidden_copied, k + 1)
                if not first:
                    pe.wait_ge(y_copied, k)
                for j in range(FK):
                    w = arena[:, bass.ds(e * WCOLS + (W2 + j * D), D)]
                    ins = pe.matmul(st[0][:, 0:D], hidden_cols[:, j, :], w, start=(j == 0), stop=(j == FK - 1))
                ins.then_inc(y_mm, 1)

            def tile(k, first=False):
                e, e_before = expert_of(k), expert_of(k - 1)
                pe.wait_ge(cols_copied, k + 1)
                up(k, e, W1, mx[0], gate_mm)
                turn_hidden(k - 1)
                return e, e_before

            turn_rows(0)
            pe.wait_ge(cols_copied, 1)
            e0 = expert_of(0)
            up(0, e0, W1, mx[0], gate_mm)
            turn_rows(1)
            up(0, e0, W3, mx[1], up_mm)

            def middle(k, first=False):
                e, e_before = tile(k)
                turn_rows(k + 1)
                up(k, e, W3, mx[1], up_mm)
                down(k - 1, e_before, first)

            middle(1, first=True)
            with pe.Fori(2, TILES - 1) as k:
                middle(k)
            e, e_before = tile(TILES - 1)
            up(TILES - 1, e, W3, mx[1], up_mm)
            down(TILES - 2, e_before)
            turn_hidden(TILES - 1)
            down(TILES - 1, e)

        @block.vector
        def _(dve):
            steps = [0]

            def own(ins):
                steps[0] += 1
                ins.then_inc(vec_step, 1)
                dve.wait_ge(vec_step, steps[0])

            for s in range(STACKS):
                dve.memset(k_stack[s][96:128, :, :].bitcast(F32), TWO_ONES).then_inc(ones_made, 1)
            dve.wait_ge(setup_mm, 1)
            dve.tensor_copy(c_cols[:, :, :].rearrange("p j b -> p (j b)"), misc2[0][:, 0:DK * B]).then_inc(setup_dve, 1)
            dve.wait_ge(c_step, 1)
            own(dve.tensor_scalar(c_exp[:, :, :], c_exp[:, :, :], 1.0, None, ALU.add))
            own(dve.reciprocal(c_silu[:, :, :], c_exp[:, :, :]))
            dve.tensor_tensor(c_silu[:, :, :], c_silu[:, :, :], c_cols[:, :, :], ALU.mult).then_inc(c_ready, 1)

            def modulation_columns():
                dve.wait_ge(setup_mm, 2)
                dve.tensor_copy(mod_rows[:, 0:D], mx[0][0:B, 0:D]).then_inc(setup_dve, 1)
                dve.tensor_scalar(mod_rows[:, D:2 * D], mx[0][0:B, D:2 * D], 1.0, None, ALU.add).then_inc(setup_dve, 1)
                dve.wait_ge(setup_mm, 3)
                dve.tensor_copy(mod_cols[:, :, :].rearrange("p n b -> p (n b)"), misc2[0][:, 0:4 * B]).then_inc(setup_dve, 1)

            def modulation_rows():
                dve.wait_ge(setup_mm, 5)
                own(dve.tensor_scalar(mod_rows[:, 4 * D:5 * D], pv[0:B, 0:D], 1.0, None, ALU.add))
                own(dve.tensor_copy(mod_rows[:, 3 * D:4 * D], mx[1][0:B, D:2 * D]))
                for n, src in enumerate((mx[1][0:B, 0:D], pv[0:B, D:2 * D])):
                    own(dve.tensor_scalar(gtmp[:, 0, :], src, 0.0, 2.0, ALU.is_ge, ALU.mult))
                    own(dve.tensor_scalar(gtmp[:, 0, :], gtmp[:, 0, :], -1.0, None, ALU.add))
                    own(dve.tensor_scalar(gtmp[:, 1, :], src, -1.0, None, ALU.mult))
                    own(dve.tensor_tensor(gtmp[:, 1, :], gtmp[:, 1, :], src, ALU.max))
                    own(dve.tensor_scalar(gtmp[:, 1, :], gtmp[:, 1, :], 0.25, None, ALU.max))
                    ins = dve.tensor_tensor(mod_rows[:, (2 + 3 * n) * D:(3 + 3 * n) * D], gtmp[:, 0, :], gtmp[:, 1, :], ALU.mult)
                    if n == 0:
                        own(ins)
                ins.then_inc(mod_ready, 1)

            for key in STEPS:
                kind, misc = key[0], bank_of(key)
                if kind == "norm_stats":
                    b = key[1]
                    dve.wait_ge(x_loaded[b], 16)
                    if b >= 1:
                        dve.wait_ge(rstd_ready, b)
                    for i in range(TT):
                        own(dve.bn_stats(stats[:, i, :], xs[:, b * TT + i, :]))
                        ins = dve.bn_aggr(moments[:, i, :], stats[:, i, :])
                        if i < TT - 1:
                            own(ins)
                    ins.then_inc(stats_ready, 1)
                elif kind == "norm_rows":
                    b = key[1]
                    dve.wait_ge(rstd_ready, b + 1)
                    if b >= 1:
                        wait_filled(dve, ("h_cols", b - 1, 1))
                    for i in range(TT):
                        dve.tensor_scalar(xn[:, i, :], xs[:, b * TT + i, :], moments[:, i, 0:1], rstd[:, i:i + 1],
                                          ALU.subtract, ALU.mult).then_inc(xn_ready, 1)
                    if b == 0:
                        modulation_columns()
                elif kind == "split" and key[1:] == (0, 1):
                    modulation_rows()
                elif kind == "project":
                    _, u, w = key
                    n = 2 * u + w
                    dve.wait_ge(high_ready, n + 1)
                    if n >= 2:
                        dve.wait_ge(low_ready, n - 1)
                    dve.scalar_tensor_tensor(out=rest[w], in0=misc[:, :], scalar=(HD ** -0.5, 1.0)[w],
                                             in1=parts[w][:, 0, :], op0=ALU.mult, op1=ALU.subtract).then_inc(dve_evac, 1)
                elif kind == "max_fill":
                    _, u, n = key
                    i, h0, nh = max_fill(n)
                    w = (i + 1) * P
                    f = FILLS * u + n
                    if n == 0 and u >= 2:
                        wait_filled(dve, ("max_rows", u - 2))
                    dve.wait_ge(mx_filled, f + 1)
                    dve.tensor_reduce(row_max[:, u % 2, i, h0:h0 + nh],
                                      mx[f % 2][:, 0:nh * w].rearrange("p (h s) -> p h s", h=nh), AX_X, ALU.max).then_inc(mx_drained, 1)
                elif kind == "max_rows":
                    u = key[1]
                    dve.wait_ge(mhigh_ready, u + 1)
                    if u >= 1:
                        dve.wait_ge(mlow_ready, u)
                    dve.scalar_tensor_tensor(out=max_rest[:, :], in0=misc[0:HU, :], scalar=-1.0,
                                             in1=max_parts[:, 0, :], op0=ALU.mult, op1=ALU.subtract).then_inc(dve_evac, 1)
                elif kind == "z_rows":
                    t = key[1]
                    wait_filled(dve, key)
                    z = misc[:, :].rearrange("p (h d) -> p h d", h=NH)
                    own(dve.reciprocal(z_recip[:, :], z[:, :, HD]))
                    dve.tensor_tensor(zn[:, :, :], z[:, :, 0:HD], z_recip[:, :].unsqueeze(2).to_broadcast([P, NH, HD]),
                                      ALU.mult).then_inc(dve_evac, 1)
                elif kind == "out_rows":
                    t = key[1]
                    wait_filled(dve, key)
                    dve.tensor_tensor(xs[:, t, :], misc[:, 0:D], xs[:, t, :], ALU.add).then_inc(dve_evac, 1)
                    wait_evacuated(dve, key)
                    if t >= 2:
                        dve.wait_ge(rstd2_ready, t - 1)
                    own(dve.bn_stats(stats2[:, :], xs[:, t, :]))
                    dve.bn_aggr(moments2[:, t % 2, :], stats2[:, :]).then_inc(stats2_ready, 1)
                elif kind == "norm2":
                    t = key[1]
                    b, i = t // TT, t % TT
                    dve.wait_ge(rstd2_ready, t + 1)
                    if b >= 1:
                        dve.wait_ge(scattered[i], 16 * 2 * b)
                    dve.tensor_scalar(h2x[:, i, 0, 0:D], xs[:, t, :], moments2[:, t % 2, 0:1], rstd2[:, t % 2:t % 2 + 1],
                                      ALU.subtract, ALU.mult).then_inc(xn2_ready, 1)
                elif kind == "gate":
                    b = key[1]
                    wait_evacuated(dve, ("router", b * TT + TT - 1))
                    own(dve.tensor_reduce(gate_s[:, 0, :], logits[:, :, :], AX_X, ALU.max))
                    dve.tensor_tensor(gate_t[:, :, :], logits[:, :, :], gate_s[:, 0, :].unsqueeze(2).to_broadcast([P, TT, E]),
                                      ALU.subtract).then_inc(shifted, 1)
                elif kind == "choose":
                    _, b, part = key
                    wide = [P, TT, E]
                    rev = rev_e[:, :].unsqueeze(1).to_broadcast(wide)
                    if part == 0:
                        dve.wait_ge(gate_exped, b + 1)
                        if b == 0:
                            dve.wait_ge(pool_const, CONSTS)
                        own(dve.tensor_reduce(gate_s[:, 1, :], gate_exp[:, :, :], AX_X, ALU.add))
                        own(dve.reciprocal(gate_s[:, 2, :], gate_s[:, 1, :]))
                        own(dve.tensor_tensor(gate_p[:, :, :], gate_exp[:, :, :], gate_s[:, 2, :].unsqueeze(2).to_broadcast(wide), ALU.mult))
                    elif part < 3:
                        n = part - 1
                        own(dve.tensor_reduce(top_w[:, n, :], gate_p[:, :, :], AX_X, ALU.max))
                        own(dve.tensor_tensor(gate_t[:, :, :], gate_p[:, :, :], top_w[:, n, :].unsqueeze(2).to_broadcast(wide), ALU.is_equal))
                        own(dve.tensor_tensor(gate_t[:, :, :], gate_t[:, :, :], rev, ALU.mult))
                        own(dve.tensor_reduce(gate_s[:, 3, :], gate_t[:, :, :], AX_X, ALU.max))
                        own(dve.tensor_tensor(hot[:, n], rev, gate_s[:, 3, :].unsqueeze(2).to_broadcast(wide), ALU.is_equal))
                        if n == 0:
                            own(dve.scalar_tensor_tensor(out=gate_p[:, :, :], in0=hot[:, 0], scalar=-2.0, in1=gate_p[:, :, :],
                                                         op0=ALU.mult, op1=ALU.add))
                    else:
                        own(dve.tensor_tensor(chosen[:, b * TT:(b + 1) * TT, :], hot[:, 0], hot[:, 1], ALU.add))
                        for i in range(TT):
                            t = b * TT + i
                            ins = dve.tensor_tensor(before[:, t + 1, :], before[:, t, :], chosen[:, t, :], ALU.add)
                            if i < TT - 1:
                                own(ins)
                        ins.then_inc(chosen_ready, 1)
                elif kind == "rank":
                    b = key[1]
                    wide = [P, TT, E]
                    wait_filled(dve, key)
                    dve.tensor_tensor(rank_pos[:, :, :], misc[:, 0:TT * E].rearrange("p (i e) -> p i e", i=TT),
                                      base_e[:, :].unsqueeze(1).to_broadcast(wide), ALU.add).then_inc(dve_evac, 1)
                    wait_evacuated(dve, key)
                    for n in range(2):
                        own(dve.tensor_tensor(gate_t[:, :, :], rank_pos[:, :, :], hot[:, n], ALU.mult))
                        own(dve.tensor_reduce(pos_f[:, n, :], gate_t[:, :, :], AX_X, ALU.add))
                        own(dve.tensor_copy(h2x[:, :, n, DEST].bitcast(I32), dest[:, n, b * TT:(b + 1) * TT]))
                        own(dve.tensor_copy(h2x[:, :, n, WEIGHT], top_w[:, n, :]))
                    dve.tensor_copy(pos_i[:, :, :], pos_f[:, :, :]).then_inc(routed, 1)
            dve.wait_ge(setup_mm, 6)
            own(dve.tensor_tensor(fill_f[:, :], misc2[0][:, 0:E], part_base[:, :], ALU.add))
            own(dve.tensor_scalar(count_f[:, :], misc2[0][0:1, 0:E], float(P - 1), None, ALU.add))
            dve.tensor_copy(fill_i[:, :], fill_f[:, :]).then_inc(fill_ready, 1)
            own(dve.tensor_copy(count_i[:, :], count_f[:, :]))
            own(dve.tensor_single_scalar(count_i[:, :], count_i[:, :], 7, ALU.logical_shift_right))
            own(dve.tensor_copy(ntile[:, :], count_i[:, :]))
            own(dve.tensor_copy(ends[:, 0, :], ntile[:, :]))
            for n, d in enumerate((1, 2, 4)):
                own(dve.tensor_copy(ends[:, n + 1, 0:d], ends[:, n, 0:d]))
                own(dve.tensor_tensor(ends[:, n + 1, d:E], ends[:, n, d:E], ends[:, n, 0:E - d], ALU.add))
            end = ends[:, 3, :]
            wide = [1, TILES, E]
            own(dve.tensor_tensor(tab_a, tile_no[:, :].unsqueeze(2).to_broadcast(wide),
                                  end.unsqueeze(1).to_broadcast(wide), ALU.is_ge))
            own(dve.tensor_tensor(tab_b, tab_a, ntile[:, :].unsqueeze(1).to_broadcast(wide), ALU.mult))
            own(dve.tensor_reduce(tab_v[:, 0, :], tab_a, AX_X, ALU.add))
            own(dve.tensor_reduce(tab_v[:, 1, :], tab_b, AX_X, ALU.add))
            own(dve.tensor_tensor(tab_v[:, 2, :], tile_no[:, :], tab_v[:, 1, :], ALU.subtract))
            own(dve.tensor_scalar(tab_v[:, 2, :], tab_v[:, 2, :], float(P), None, ALU.mult))
            own(dve.scalar_tensor_tensor(out=tab_v[:, 3, :], in0=tab_v[:, 0, :], scalar=float(REGION), in1=tab_v[:, 2, :],
                                         op0=ALU.mult, op1=ALU.add))
            own(dve.tensor_scalar(tab_v[:, 3, :], tab_v[:, 3, :], float(NULL_ROW), None, ALU.min))
            own(dve.tensor_scalar(tab_v[:, 0, :], tab_v[:, 0, :], float(E - 1), None, ALU.min))
            own(dve.tensor_copy(table[:, 0, :], tab_v[:, 0, :]))
            dve.tensor_copy(table[:, 1, :], tab_v[:, 3, :]).then_inc(table_ready, 1)

            def rows_out(k, turn, first=False):
                dve.wait_ge(xg_turned, k + 1)
                dve.tensor_copy(xg_cols.rearrange("p j t -> p (j t)"), misc2[0][:, 0:D]).then_inc(cols_copied, 1)
                if not first:
                    dve.wait_ge(y_stored, 16 * (k - 3))
                dve.tensor_copy(tail[turn].bitcast(I32), xg[:, DEST:DEST + 2].bitcast(I32)).then_inc(tail_copied, 1)

            def gated(k):
                dve.wait_ge(silu_done, k + 1)
                dve.wait_ge(up_mm, k + 1)
                dve.tensor_tensor(hidden, silu_sb, mx[1][:, :], ALU.mult).then_inc(hidden_ready, 1)

            def tile(k, turn, first=False):
                gated(k)
                rows_out(k + 1, (turn + 1) % 4, first)

            rows_out(0, 0, first=True)
            for k in range(3):
                tile(k, k, first=True)
            with dve.Fori(3, TILES - 4, 4) as k:
                for n in range(4):
                    tile(k + n, (3 + n) % 4)
            for k in range(TILES - 4, TILES - 1):
                tile(k, k % 4)
            gated(TILES - 1)

            dve.wait_ge(y_loaded, 32)
            for b in range(B):
                tiles = slice(b * TT, (b + 1) * TT)
                own(dve.tensor_tensor(ya[:, tiles, :], ya[:, tiles, :], yb[:, tiles, :], ALU.add))
                own(dve.tensor_tensor(ya[:, tiles, :], ya[:, tiles, :],
                                      mods[:, b, 3, :].unsqueeze(1).to_broadcast([P, TT, D]), ALU.mult))
                dve.tensor_tensor(xs[:, tiles, :], xs[:, tiles, :], ya[:, tiles, :], ALU.add).then_inc(out_ready, 1)


def kernel(**inputs):
    import numpy as np
    import concourse.bacc as bacc
    from concourse.bass_utils import run_bass_kernel_spmd

    def laid(name, turn=False):
        a = np.asarray(inputs[name])
        return np.ascontiguousarray(a.T if turn else a)

    arrays = {
        "x": laid("L0_attn_x"),
        "wq": laid("L0_attn_Wq", True),
        "wk": laid("L0_attn_Wk", True),
        "wv": laid("L0_attn_Wv", True),
        "wo": laid("L0_attn_Wo", True),
        "gate_w": laid("L0_ffn_gate_w"),
        "w1": laid("L0_ffn_w1"),
        "w3": laid("L0_ffn_w3"),
        "w2": laid("L0_ffn_w2"),
        "c": laid("L0_c"),
        "wmod": laid("L0_wmod"),
    }
    nc = bacc.Bacc("TRN2", target_bir_lowering=False, num_devices=1)
    aps = [nc.dram_tensor(n, a.shape, mybir.dt.from_np(a.dtype), kind="ExternalInput").ap() for n, a in arrays.items()]
    out = nc.dram_tensor("out", [B, T, D], F32, kind="ExternalOutput").ap()
    build(nc, *aps, out)
    r = run_bass_kernel_spmd(nc, [arrays], core_ids=[0])
    return r.results[0]["out"]
```

```python
from contextlib import ExitStack

import concourse.bass as bass
from concourse import mybir

F32 = mybir.dt.float32
BF16 = mybir.dt.bfloat16
I32 = mybir.dt.int32
ALU = mybir.AluOpType
ACT = mybir.ActivationFunctionType
AX_X = mybir.AxisListType.X

P = 128
B, T, D = 4, 512, 256
NH, HD = 16, 16
E, F = 8, 512
N = B * T
DK = D // P
FK = F // P
TT = T // P
NT = N // P
EPS = 1e-5

HU = NH // 2
UNITS = B * 2
HG = 4
GROUPS = UNITS * HU // HG
NTERMS = 6
KS = NTERMS * HD
KB = KS + 3
Q_PART = (0, 0, 0, 1, 1, 2)
K_PART = (0, 1, 2, 0, 1, 0)
STACKS = 3

REGION = N + P
ROW = D + 2
DEST, WEIGHT = D, D + 1
NULL_ROW = E * REGION
HS_ROWS = E * REGION + P
TILES = 2 * N // P + E - 1
FIRST = 16
assert FIRST * P <= 2 * (N - T) - E * (P - 1)
PIECE = 2
PIECES = NT // PIECE
PEELED = 6
WCOLS = 2 * DK * F + FK * D
EARLY = 1
W1, W3, W2 = 0, DK * F, 2 * DK * F
NEG = -3.0e38
TWO_ONES = (1 << 23 | 0x3F80) / 2.0 ** 23


def scatters(b):
    return [("scatter", b, i, n) for i in range(TT) for n in range(2)]


WHEN = {
    "maxima": ((-0.163, 0.523), (-0.452, 0.319), None, (0.552, 0.552)),
    "max_rows": ((0.56, 0.723), (0.437, 0.437), None, (0.36, 1.127)),
    "max_split": ((0.448, 0.894), (0.172, 1.026), None, (0.74, 0.845)),
    "project": ((0.005, 0.015), (-0.735, -0.601), (-0.31, -0.095), (-0.293, -0.149)),
    "split": ((0.125, 0.209), (-0.418, -0.137), (-0.276, 0.26), (0.147, 0.292)),
    "values": ((0.07, 0.313), None, (0.509, 0.704), None),
    "norm_stats": (None, (0.003, 0.763), None, (-1.79, -1.388)),
    "norm_rows": (None, (0.586, 1.02), None, (-0.498, -0.396)),
    "h_cols": (None, (0.916, 0.916), None, (0.224, 0.241)),
    "back": ((0.107, 0.839), (-0.572, 0.27)),
    "gate": ((-0.788, -0.681), None),
    "choose": ((-0.636, -0.062), None),
    "rank": ((-0.213, 0.118), None),
    "scatter": ((0.161, 0.238), (0.422, 0.545)),
    "value_sum": ((0.214, 0.232), (0.175, 0.098)),
    "constants": (None, None, None, (-0.539, 0.064)),
    "ones": (None, None, None, (0.164, 1.16)),
    "modulation": (None, None, (-0.038, 0.48), None),
    "mods_out": (None, None, (0.939, 1.497), None),
    "first_tiles": ((-0.066, 0.603), None),
    "last": ((0.4, 1.197), (1, 1)),
}


def attention_steps():
    timed = []

    def spread(s, where, steps):
        if isinstance(where, str):
            where = WHEN[where][s % 2 + (2 if s < 0 else 0)]
        a, b = where
        for j, step in enumerate(steps):
            timed.append((s + a + (b - a) * (j + 0.5) / len(steps), len(timed), step))

    for s in range(-2, UNITS + 1):
        if 0 <= s < UNITS:
            spread(s, (0, 1), [("score", 2 * s + n // SLOTS, n % SLOTS) for n in range(2 * SLOTS)])
            for g in range(2):
                for k in range(TT):
                    first, last = WHEN["value_sum"][g]
                    at = (g + (LAST_SLOT[k] + 1) / SLOTS) / 2 + first + (last - first) * k / (TT - 1)
                    spread(s, (at, at), [("value_sum", 2 * s + g, k)])
        u = s + 1
        if 0 <= u < UNITS:
            spread(s, "maxima", [("max_fill", u, n) for n in range(FILLS)])
            spread(s, "max_rows", [("max_rows", u)])
            spread(s, "max_split", [("max_split", u)])
        u = s + 2
        if u < UNITS:
            spread(s, "project", [("project", u, 0), ("project", u, 1)])
            spread(s, "split", [("split", u, 0), ("split", u, 1)])
            if u % 2 == 0:
                spread(s, "values", [("values", u // 2, i) for i in range(TT)])
        b = (s + 3) // 2
        if s % 2 and b < B:
            spread(s, "norm_stats", [("norm_stats", b)])
            spread(s, "norm_rows", [("norm_rows", b)])
            spread(s, "h_cols", [("h_cols", b, 0), ("h_cols", b, 1)])
        if s >= 2:
            b, half = (s - 2) // 2, s % 2
            first = b * TT + 2 * half
            last = s == UNITS
            tiles = range(b * TT, (b + 1) * TT) if last else (first, first + 1)
            kinds = ("z_rows", "z_cols", "out_rows", "norm2", "h2_cols", "router")
            lag = WHEN["last"][1][0 if last else 1]
            back = []
            for n in range(lag * (len(tiles) - 1) + len(kinds)):
                for j, t in enumerate(tiles):
                    if 0 <= n - lag * j < len(kinds):
                        back.append((kinds[n - lag * j], t))
            spread(s, WHEN["last"][0] if last else "back", back)
        if s >= 4 and s % 2 == 0:
            b = s // 2 - 2
            spread(s, "gate", [("gate", b)])
            spread(s, "choose", [("choose", b, n) for n in range(4)])
            spread(s, "rank", [("rank", b)])
            for half in range(2):
                spread(s, WHEN["scatter"][half], scatters(b)[half * TT:(half + 1) * TT])
        if s == UNITS:
            spread(s, "first_tiles", [("counts", 0), ("table", 0)])
            spread(s, (0.1, 0.1), [("weights", e) for e in (6, 7)])
        if s == -1:
            spread(s, "constants", [("constants", 1)])
            spread(s, "ones", [("ones", n) for n in range(STACKS)])
        if s == -2:
            spread(s, "modulation", [("modulation",)])
            spread(s, "mods_out", [("mods_out",)])
        if s == UNITS - 2:
            spread(s, (0, 0), [("weights", e) for e in range(EARLY, 4)])
        if s == UNITS - 1:
            spread(s, (0, 0), [("weights", e) for e in range(4, 6)])
    b = B - 1
    return ([("norm_stats", 0), ("norm_rows", 0), ("h_cols", 0, 0), ("h_cols", 0, 1), ("constants", 0)] +
            [step for *_, step in sorted(timed)] +
            [("gate", b), ("tile", 0), ("choose", b, 0), ("choose", b, 1), ("tile", 1),
             ("choose", b, 2), ("choose", b, 3), ("tile", 2), ("counts", 1), ("rank", b), ("tile", 3)] +
            scatters(b)[:TT] + [("table", 1), ("tile", 4)] + scatters(b)[TT:] + [("tile", 5)] +
            [("fill", e) for e in range(E)])


FILLS = 2 + 4 + 8 + 8


def max_fill(n):
    if n < 2:
        return 0, 4 * n, 4
    if n < 6:
        return 1, 2 * (n - 2), 2
    i = 2 + (n - 6) // HU
    return i, (n - 6) % HU, 1


SLOTS = 4 + 4 + 2 + 1
ST = 3


LAST_SLOT = (3, 7, 9, 10)


def score_slot(n):
    if n < 8:
        return n // 4, n % 4, 1
    return ((2, 0, 2), (2, 2, 2), (3, 0, 4))[n - 8]


def build(nc, x, wq, wk, wv, wo, gate_w, w1, w3, w2, c, wmod, out):
    with ExitStack() as ctx:
        def sb(name, shape, dt=F32):
            return ctx.enter_context(nc.sbuf_tensor(name, shape, dt))

        def sem(name):
            return ctx.enter_context(nc.semaphore(name))

        split_dram = nc.dram_tensor("split_dram", [UNITS, 2, P, 3, T], BF16)
        max_dram = nc.dram_tensor("max_dram", [UNITS, HU, 3, T], BF16)
        mod_dram = nc.dram_tensor("mod_dram", [B, 6 * D], F32)
        routed_dram = nc.dram_tensor("routed_dram", [HS_ROWS, ROW], F32)
        expert_dram = nc.dram_tensor("expert_dram", [2 * N + P, D], F32)

        arena = sb("arena", [P, EARLY * WCOLS + 28160 + TT * D + 4 * T])
        weights = arena[:, 0:E * WCOLS].rearrange("p (e n) -> p e n", e=E)
        place = [EARLY * WCOLS]

        def scratch(cols):
            place[0] += cols
            return arena[:, place[0] - cols:place[0]]

        h_cols = [scratch(DK * T).rearrange("p (j t) -> p j t", j=DK) for _ in range(2)]
        parts = [scratch(3 * T // 2).bitcast(BF16).rearrange("p (a t) -> p a t", a=3) for _ in range(2)]
        rest = [scratch(T) for _ in range(2)]
        xn = scratch(TT * D).rearrange("p (i d) -> p i d", i=TT)
        v_rows = [scratch(TT * NH * 32).rearrange("p (i h d) -> p i h d", i=TT, h=NH)]
        stacks = [[scratch(HU * T // 2).bitcast(BF16).rearrange("p (h t) -> p h t", h=HU) for _ in range(2)]
                  for _ in range(STACKS)]
        turns = [(UNITS - STACKS + i) % STACKS for i in range(STACKS)]
        q_stack = [stacks[turns.index(i)][0] for i in range(STACKS)]
        k_stack = [stacks[turns.index(i)][1] for i in range(STACKS)]
        probs_all = scratch(HG * (512 + 384 + 256 + 128))
        v_rows.append(scratch(TT * NH * 32).rearrange("p (i h d) -> p i h d", i=TT, h=NH))
        z_all = [scratch(4 * T) for _ in range(2)]
        z_cols = [z.rearrange("p (g t) -> p g t", g=4) for z in z_all]
        tab_a = z_all[0][0:1, 0:TILES * E].rearrange("p (k e) -> p k e", e=E)
        tab_b = z_all[0][0:1, TILES * E:2 * TILES * E].rearrange("p (k e) -> p k e", e=E)
        probs, at = [], 0
        for k in range(TT):
            w = T - k * P
            probs.append(probs_all[:, at:at + HG * w].rearrange("p (h t) -> p h t", h=HG))
            at += HG * w
        wmod_sb = probs_all[:, 0:DK * 6 * D].rearrange("p (j n) -> p j n", j=DK)
        mod_rows = probs_all[0:B, DK * 6 * D:DK * 6 * D + 6 * D]
        place[0] = E * WCOLS
        xg = scratch(ROW)
        place[0] += ROW % 2
        xg_cols = scratch(D).rearrange("p (j t) -> p j t", j=DK)
        silu_sb = scratch(F)
        hidden = scratch(F)
        hidden_cols = scratch(F).rearrange("p (j t) -> p j t", j=FK)
        y_rows = scratch(D)
        tail = [scratch(2) for _ in range(4)]
        ya = arena[:, 0:NT * D].rearrange("p (t d) -> p t d", t=NT)
        yb = arena[:, NT * D:2 * NT * D].rearrange("p (t d) -> p t d", t=NT)

        xs = sb("xs", [P, NT, D])
        wqk_sb = sb("wqk_sb", [P, 2, DK, D])
        wv_sb = sb("wv_sb", [P, DK, D])
        wo_sb = sb("wo_sb", [P, DK, D])
        wog = sb("wog", [P, DK, D])
        gate_sb = sb("gate_sb", [P, DK, E])
        mods = sb("mods", [P, B, 4, D])
        mod_cols = sb("mod_cols", [P, 4, B])
        h2x = sb("h2x", [P, TT, 2, ROW])
        h2_cols = sb("h2_cols", [P, DK, P])
        zn = sb("zn", [P, NH, HD])
        zn_cols = sb("zn_cols", [P, DK, P])
        z_recip = sb("z_recip", [P, NH])
        ident = sb("ident", [P, P])
        identb = sb("identb", [P, P], BF16)
        causal = sb("causal", [P, P], BF16)
        earlier = sb("earlier", [P, P], BF16)
        onesb = sb("onesb", [P, P], BF16)
        c_sb = sb("c_sb", [B, D])
        c_cols = sb("c_cols", [P, DK, B])
        c_exp = sb("c_exp", [P, DK, B])
        c_silu = sb("c_silu", [P, DK, B])
        gtmp = sb("gtmp", [B, 2, D])
        stats = sb("stats", [P, TT, 6])
        moments = sb("moments", [P, TT, 2])
        rstd = sb("rstd", [P, TT])
        stats2 = sb("stats2", [P, 6])
        moments2 = sb("moments2", [P, 2, 2])
        rstd2 = sb("rstd2", [P, 2])
        minus_half = sb("minus_half", [P, TT])
        row_max = sb("row_max", [P, 2, TT, HU])
        max_parts = sb("max_parts", [HU, 3, T], BF16)
        max_rest = sb("max_rest", [HU, T])
        logits = sb("logits", [P, TT, E])
        gate_exp = sb("gate_exp", [P, TT, E])
        gate_p = sb("gate_p", [P, TT, E])
        gate_t = sb("gate_t", [P, TT, E])
        hot = sb("hot", [P, 2, TT, E])
        gate_s = sb("gate_s", [P, 4, TT])
        top_w = sb("top_w", [P, 2, TT])
        chosen = sb("chosen", [P, NT, E], BF16)
        before = sb("before", [P, NT + 1, E], BF16)
        rank_pos = sb("rank_pos", [P, TT, E])
        pos_f = sb("pos_f", [P, 2, TT])
        pos_i = sb("pos_i", [P, 2, TT], I32)
        rev_e = sb("rev_e", [P, E])
        base_e = sb("base_e", [P, E])
        part_base = sb("part_base", [P, E])
        dest = sb("dest", [P, 2, NT], I32)
        null_rows = sb("null_rows", [P, ROW])
        fill_f = sb("fill_f", [P, E])
        fill_i = sb("fill_i", [P, E], I32)
        count_f = sb("count_f", [1, E])
        count_i = sb("count_i", [1, E], I32)
        ntile = sb("ntile", [1, E])
        ends = sb("ends", [1, 4, E])
        took = sb("took", [1, E])
        tile_no = sb("tile_no", [1, TILES])
        tab_v = sb("tab_v", [1, 6, TILES])
        table = sb("table", [1, 2, TILES], I32)

        st = [ctx.enter_context(nc.psum_tensor(f"st{i}", [P, 512], F32)) for i in range(ST)]
        mx = [ctx.enter_context(nc.psum_tensor(f"mx{i}", [P, 512], F32)) for i in range(2)]
        pv = ctx.enter_context(nc.psum_tensor("pv", [P, 512], F32))
        misc2 = [ctx.enter_context(nc.psum_tensor(f"misc{i}", [P, 512], F32)) for i in range(2)]

        x_loaded = [sem(f"x_loaded{b}") for b in range(B)]
        small_loaded = sem("small_loaded")
        wmod_loaded = [sem(f"wmod_loaded{n}") for n in range(3)]
        attn_w_loaded = sem("attn_w_loaded")
        first_w_loaded = sem("first_w_loaded")
        last_w_loaded = sem("last_w_loaded")
        pool_const = sem("pool_const")
        ones_made = sem("ones_made")
        mod_ready = sem("mod_ready")
        mod_stored = sem("mod_stored")
        mods_loaded = sem("mods_loaded")
        c_step = sem("c_step")
        c_ready = sem("c_ready")
        setup_mm = sem("setup_mm")
        setup_dve = sem("setup_dve")
        wog_ready = sem("wog_ready")
        stats_ready = sem("stats_ready")
        rstd_ready = sem("rstd_ready")
        xn_ready = sem("xn_ready")
        misc_filled = sem("misc_filled")
        act_evac = sem("act_evac")
        dve_evac = sem("dve_evac")
        high_ready = sem("high_ready")
        mid_ready = sem("mid_ready")
        low_ready = sem("low_ready")
        parts_stored = [sem(f"parts_stored{w}") for w in range(2)]
        stack_loaded = [sem(f"stack_loaded{i}") for i in range(STACKS)]
        mx_filled = sem("mx_filled")
        mx_drained = sem("mx_drained")
        mhigh_ready = sem("mhigh_ready")
        mmid_ready = sem("mmid_ready")
        mlow_ready = sem("mlow_ready")
        max_stored = sem("max_stored")
        max_loaded = [sem(f"max_loaded{i}") for i in range(STACKS)]
        st_filled = sem("st_filled")
        exp_done = sem("exp_done")
        pv_done = sem("pv_done")
        z_copied = sem("z_copied")
        stats2_ready = sem("stats2_ready")
        rstd2_ready = sem("rstd2_ready")
        xn2_ready = sem("xn2_ready")
        h2_ready = sem("h2_ready")
        h2_copied = sem("h2_copied")
        shifted = sem("shifted")
        gate_exped = sem("gate_exped")
        chosen_ready = sem("chosen_ready")
        routed = sem("routed")
        scattered = [sem(f"scattered{i}") for i in range(TT)]
        filled = sem("filled")
        fill_ready = sem("fill_ready")
        table_ready = sem("table_ready")
        null_stored = sem("null_stored")
        vec_step = sem("vec_step")
        pool_step = sem("pool_step")
        xg_loaded = sem("xg_loaded")
        xg_turned = sem("xg_turned")
        cols_copied = sem("cols_copied")
        tail_copied = sem("tail_copied")
        gate_mm = sem("gate_mm")
        up_mm = sem("up_mm")
        silu_done = sem("silu_done")
        hidden_ready = sem("hidden_ready")
        hidden_turned = sem("hidden_turned")
        hidden_copied = sem("hidden_copied")
        y_mm = sem("y_mm")
        y_copied = sem("y_copied")
        y_stored = sem("y_stored")
        store_turn = sem("store_turn")
        y_loaded = [sem(f"y_loaded{n}") for n in range(PIECES)]
        y_summed = [sem("y_summed_dve"), sem("y_summed_pool")]
        y_gated = sem("y_gated")
        out_ready = sem("out_ready")
        out_stored = sem("out_stored")

        STEPS = attention_steps()
        IDENT_MADE, CAUSAL_MADE, V0_MADE, NULL_MADE, V1_MADE, CONSTS = 2, 4, 5, 6, 7, 15
        ON_ACT = ("h_cols", "values", "z_cols", "h2_cols", "router")
        ON_DVE = ("project", "max_rows", "z_rows", "out_rows", "rank", "counts")
        use, evacs = {}, {"act": 0, "dve": 0}
        for key in STEPS:
            if key[0] in ON_ACT + ON_DVE:
                who = "act" if key[0] in ON_ACT else "dve"
                evacs[who] += 1
                use[key] = (len(use), who, evacs[who])
        use_order = sorted(use, key=lambda k: use[k][0])

        def bank_of(key):
            return misc2[use[key][0] % 2] if key in use else None

        def wait_filled(eng, key):
            eng.wait_ge(misc_filled, use[key][0] + 1)

        def wait_evacuated(eng, key):
            _, who, count = use[key]
            eng.wait_ge(act_evac if who == "act" else dve_evac, count)

        def stack_turn(u):
            return u // STACKS + 1

        block = ctx.enter_context(nc.Block())

        @block.sync
        def _(sp):
            sp.dma_start(c_sb[:, :], c).then_inc(small_loaded, 16)
            xv = x.rearrange("b (i p) d -> b p i d", p=P)
            sp.dma_start(xs[:, 0:TT, :], xv[0]).then_inc(x_loaded[0], 16)
            wmod_cols = wmod.rearrange("(j p) n -> p j n", p=P)
            sp.dma_start(wmod_sb[:, :, 0:512], wmod_cols[:, :, 0:512]).then_inc(wmod_loaded[0], 16)
            for n, w in enumerate((wq, wk)):
                sp.dma_start(wqk_sb[:, n], w.rearrange("(j p) n -> p j n", p=P)).then_inc(attn_w_loaded, 16)
            sp.dma_start(wv_sb[:, :, :], wv.rearrange("(j p) n -> p j n", p=P)).then_inc(attn_w_loaded, 16)
            sp.dma_start(wo_sb[:, :, :], wo.rearrange("(j p) n -> p j n", p=P)).then_inc(attn_w_loaded, 16)
            sp.dma_start(gate_sb[:, :, :], gate_w.rearrange("(j p) n -> p j n", p=P)).then_inc(attn_w_loaded, 16)
            for n in range(1, 3):
                sp.dma_start(wmod_sb[:, :, n * 512:(n + 1) * 512], wmod_cols[:, :, n * 512:(n + 1) * 512]).then_inc(wmod_loaded[n], 16)
            for b in range(1, B):
                sp.dma_start(xs[:, b * TT:(b + 1) * TT, :], xv[b]).then_inc(x_loaded[b], 16)

            def load_weights(e, done):
                sp.dma_start(weights[:, e, W1:W3].rearrange("p (j f) -> p j f", j=DK),
                             w1[e].rearrange("(j p) f -> p j f", p=P)).then_inc(done, 16)
                sp.dma_start(weights[:, e, W3:W2].rearrange("p (j f) -> p j f", j=DK),
                             w3[e].rearrange("(j p) f -> p j f", p=P)).then_inc(done, 16)
                sp.dma_start(weights[:, e, W2:WCOLS].rearrange("p (j d) -> p j d", j=FK),
                             w2[e].rearrange("(j p) d -> p j d", p=P)).then_inc(done, 16)

            early = 0
            for key in STEPS:
                if key == ("constants", 1):
                    sp.wait_ge(pool_const, NULL_MADE)
                    sp.dma_start(routed_dram[NULL_ROW:NULL_ROW + P, :], null_rows[:, :]).then_inc(null_stored, 16)
                if key[0] == "weights":
                    e = key[1]
                    if e < 4:
                        sp.wait_ge(pv_done, 4 * (GROUPS - 4))
                    elif e < 6:
                        sp.wait_ge(pv_done, 4 * (GROUPS - 2))
                    else:
                        sp.wait_ge(pv_done, 4 * GROUPS)
                    load_weights(e, last_w_loaded)
                if key[0] == "mods_out":
                    sp.wait_ge(mod_ready, 1)
                    sp.dma_start(mod_dram[:, :], mod_rows).then_inc(mod_stored, 16)
                    sp.wait_ge(mod_stored, 16)
                    sp.dma_start(mods[:, :, :, :].rearrange("p b m d -> p b (m d)"),
                                 mod_dram[:, 2 * D:6 * D].partition_broadcast(P)).then_inc(mods_loaded, 16)
                if key[0] == "split":
                    _, u, w = key
                    sp.wait_ge(low_ready, 2 * u + w + 1)
                    sp.dma_start(split_dram[u, w], parts[w]).then_inc(parts_stored[w], 16)
                    if w == 1:
                        for v in range(2):
                            sp.wait_ge(parts_stored[v], 16 * (u + 1))
                            if u >= STACKS:
                                sp.wait_ge(st_filled, 2 * SLOTS * (u - STACKS + 1))
                            stack = (q_stack, k_stack)[v][u % STACKS]
                            for g in range(NTERMS):
                                part = (Q_PART, K_PART)[v][g]
                                src = split_dram[u, v, :, part, :].rearrange("(h d) t -> d h t", d=HD)
                                sp.dma_start(stack[g * HD:(g + 1) * HD, :, :], src).then_inc(stack_loaded[u % STACKS], 16)
                    if early < EARLY and u == 1 and w == 1:
                        load_weights(early, first_w_loaded)
                        early += 1
                if key[0] == "max_split":
                    u = key[1]
                    sp.wait_ge(mlow_ready, u + 1)
                    sp.dma_start(max_dram[u], max_parts[:, :, :]).then_inc(max_stored, 16)
                    sp.wait_ge(max_stored, 16 * (u + 1))
                    sp.dma_start(q_stack[u % STACKS][KS:KB, :, :],
                                 max_dram[u].rearrange("h a t -> a h t")).then_inc(max_loaded[u % STACKS], 16)
            sp.wait_ge(table_ready, 1)
            for i in range(TT):
                sp.wait_ge(scattered[i], 16 * 2 * (B - 1))
            sp.wait_ge(pv_done, 4 * GROUPS)

            def load_rows(k, first=False):
                row = sp.value_load(table[0:1, 1, bass.ds(k, 1)], min_val=0, max_val=NULL_ROW)
                if not first:
                    sp.wait_ge(tail_copied, k)
                sp.dma_start(xg, routed_dram[bass.ds(row, P), :]).then_inc(xg_loaded, 16)

            load_rows(0, first=True)
            with sp.Fori(1, FIRST) as k:
                load_rows(k)
            sp.wait_ge(table_ready, 2)
            for i in range(TT):
                sp.wait_ge(scattered[i], 16 * 2 * B)
            sp.wait_ge(filled, 16 * E)
            sp.wait_ge(null_stored, 16)
            with sp.Fori(FIRST, TILES) as k:
                load_rows(k)
            sp.wait_ge(y_stored, 16 * TILES)
            for n in range(PIECES):
                for y, first in ((ya, 0), (yb, N)):
                    rows = expert_dram[first + n * PIECE * P:first + (n + 1) * PIECE * P, :]
                    sp.dma_start(y[:, n * PIECE:(n + 1) * PIECE, :],
                                 rows.rearrange("(t p) d -> p t d", p=P)).then_inc(y_loaded[n], 16)
            outv = out.rearrange("b (i p) d -> p (b i) d", p=P)
            for n in range(PIECES):
                sp.wait_ge(out_ready, n + 1)
                tiles = slice(n * PIECE, (n + 1) * PIECE)
                sp.dma_start(outv[:, tiles, :], xs[:, tiles, :]).then_inc(out_stored, 16)
            sp.wait_ge(out_stored, 16 * PIECES)

        @block.gpsimd
        def _(pool):
            steps = [0]

            def own(ins):
                steps[0] += 1
                ins.then_inc(pool_step, 1)
                pool.wait_ge(pool_step, steps[0])

            consts = [0]

            def const(ins):
                consts[0] += 1
                ins.then_inc(pool_const, 1)
                pool.wait_ge(pool_const, consts[0])

            def made(count):
                assert consts[0] == count

            const(pool.memset(minus_half[:, :], -0.5))
            own(pool.memset(ident[:, :], 0.0))
            const(pool.affine_select(out=ident[:, :], in_=ident[:, :], compare_op=ALU.not_equal, fill=1.0, base=0,
                                     pattern=[[-1, P]], channel_multiplier=1))
            made(IDENT_MADE)
            const(pool.tensor_copy(identb[:, :], ident[:, :]))

            own(pool.memset(causal[:, :], 0.0))
            const(pool.affine_select(out=causal[:, :], in_=causal[:, :], compare_op=ALU.is_ge, fill=NEG, base=0,
                                     pattern=[[-1, P]], channel_multiplier=1))
            made(CAUSAL_MADE)

            def early_constants():
                own(pool.memset(v_rows[0], 0.0))
                const(pool.memset(v_rows[0][:, :, :, HD:HD + 1], 1.0))
                made(V0_MADE)
                own(pool.memset(null_rows[:, :], 0.0))
                const(pool.iota(null_rows[:, DEST:DEST + 1].bitcast(I32), pattern=[[0, 1]], base=2 * N,
                                channel_multiplier=1))
                made(NULL_MADE)

            def late_constants():
                own(pool.memset(v_rows[1], 0.0))
                const(pool.memset(v_rows[1][:, :, :, HD:HD + 1], 1.0))
                made(V1_MADE)
                own(pool.memset(earlier[:, :], 1.0))
                const(pool.affine_select(out=earlier[:, :], in_=earlier[:, :], compare_op=ALU.is_gt, fill=0.0, base=0,
                                         pattern=[[1, P]], channel_multiplier=-1))
                const(pool.memset(onesb[:, :], 1.0))
                const(pool.iota(rev_e[:, :], pattern=[[-1, E]], base=E, channel_multiplier=0,
                                allow_small_or_imprecise_dtypes=True))
                const(pool.iota(base_e[:, :], pattern=[[REGION, E]], base=0, channel_multiplier=0,
                                allow_small_or_imprecise_dtypes=True))
                const(pool.iota(part_base[:, :], pattern=[[REGION, E]], base=0, channel_multiplier=1,
                                allow_small_or_imprecise_dtypes=True))
                const(pool.iota(dest[:, :, :], pattern=[[N, 2], [P, NT]], base=0, channel_multiplier=1))
                const(pool.iota(tile_no[:, :], pattern=[[1, TILES]], base=0, channel_multiplier=0,
                                allow_small_or_imprecise_dtypes=True))
                const(pool.memset(before[:, 0, :], 0.0))
                made(CONSTS)

            def store_rows(k, turn):
                pool.wait_ge(y_copied, k + 1)
                pool.sem_inc(store_turn, 1)
                pool.indirect_dma_start(
                    out=expert_dram[:, :],
                    out_offset=bass.IndirectOffsetOnAxis(ap=tail[turn][:, 0:1].bitcast(I32), axis=0),
                    in_=y_rows, in_offset=None).then_inc(y_stored, 16)

            for key in STEPS:
                kind = key[0]
                if kind == "norm_stats":
                    b = key[1]
                    pool.wait_ge(stats_ready, b + 1)
                    own(pool.tensor_scalar(rstd[:, :], moments[:, :, 1], EPS, None, ALU.add))
                    pool.tensor_tensor(rstd[:, :], rstd[:, :], minus_half[:, :], ALU.pow).then_inc(rstd_ready, 1)
                elif kind == "split":
                    _, u, w = key
                    n = 2 * u + w
                    pool.wait_ge(mid_ready, n + 1)
                    pool.tensor_tensor(parts[w][:, 2, :], rest[w], parts[w][:, 1, :], ALU.subtract).then_inc(low_ready, 1)
                elif kind == "constants":
                    (early_constants, late_constants)[key[1]]()
                elif kind == "max_split":
                    u = key[1]
                    pool.wait_ge(mmid_ready, u + 1)
                    pool.tensor_tensor(max_parts[:, 2, :], max_rest[:, :], max_parts[:, 1, :],
                                       ALU.subtract).then_inc(mlow_ready, 1)
                elif kind == "z_rows" and key[1] % TT == 0:
                    b = key[1] // TT
                    if b == 0:
                        pool.wait_ge(mods_loaded, 16)
                        pool.wait_ge(attn_w_loaded, 80)
                    else:
                        wait_filled(pool, ("out_rows", b * TT - 1))
                    pool.tensor_tensor(wog[:, :, :], wo_sb[:, :, :],
                                       mods[:, b, 0, :].unsqueeze(1).to_broadcast([P, DK, D]), ALU.mult).then_inc(wog_ready, 1)
                elif kind == "out_rows":
                    t = key[1]
                    pool.wait_ge(stats2_ready, t + 1)
                    own(pool.tensor_scalar(rstd2[:, t % 2:t % 2 + 1], moments2[:, t % 2, 1:2], EPS, None, ALU.add))
                    pool.tensor_tensor(rstd2[:, t % 2:t % 2 + 1], rstd2[:, t % 2:t % 2 + 1], minus_half[:, 0:1],
                                       ALU.pow).then_inc(rstd2_ready, 1)
                elif kind == "norm2":
                    t = key[1]
                    b, i = t // TT, t % TT
                    row = h2x[:, i, 0, 0:D]
                    pool.wait_ge(xn2_ready, t + 1)
                    own(pool.tensor_tensor(row, row, mods[:, b, 2, :], ALU.mult))
                    pool.tensor_tensor(row, row, mods[:, b, 1, :], ALU.add).then_inc(h2_ready, 1)
                elif kind == "tile" and key[1] >= 1:
                    store_rows(key[1] - 1, (key[1] - 1) % 4)
                elif kind == "fill":
                    e = key[1]
                    pool.wait_ge(fill_ready, 1)
                    pool.indirect_dma_start(
                        out=routed_dram[:, :], out_offset=bass.IndirectOffsetOnAxis(ap=fill_i[:, e:e + 1], axis=0),
                        in_=null_rows[:, :], in_offset=None).then_inc(filled, 16)
                elif kind == "scatter":
                    _, b, i, n = key
                    pool.wait_ge(routed, b + 1)
                    pool.wait_ge(h2_copied, (b + 1) * TT)
                    pool.indirect_dma_start(
                        out=routed_dram[:, :], out_offset=bass.IndirectOffsetOnAxis(ap=pos_i[:, n, i:i + 1], axis=0),
                        in_=h2x[:, i, n, :], in_offset=None).then_inc(scattered[i], 16)
            with pool.Fori(PEELED - 1, TILES - 2, 4) as k:
                for n in range(4):
                    store_rows(k + n, (PEELED - 1 + n) % 4)
            for k in range(TILES - 2, TILES):
                store_rows(k, k % 4)
            for n in range(1, PIECES, 2):
                tiles = slice(n * PIECE, (n + 1) * PIECE)
                pool.wait_ge(y_loaded[n], 32)
                pool.tensor_tensor(ya[:, tiles, :], ya[:, tiles, :], yb[:, tiles, :], ALU.add).then_inc(y_summed[1], 1)

        @block.scalar
        def _(act):
            act.wait_ge(setup_dve, 1)
            act.activation(c_exp[:, :, :], c_cols[:, :, :], ACT.Exp, scale=-1.0).then_inc(c_step, 1)
            def silu(k):
                act.wait_ge(gate_mm, k + 1)
                act.activation(silu_sb, mx[0][:, :], ACT.Silu).then_inc(silu_done, 1)

            def hidden_out(k):
                act.wait_ge(hidden_turned, k + 1)
                act.activation(hidden_cols.rearrange("p j t -> p (j t)"), pv[:, :], ACT.Copy).then_inc(hidden_copied, 1)

            def y_out(k, turn, first=False):
                if not first:
                    act.wait_ge(y_stored, 16 * k)
                act.wait_ge(y_mm, k + 1)
                act.activation(y_rows, st[0][:, 0:D], ACT.Copy, scale=tail[turn][:, 1:2]).then_inc(y_copied, 1)

            def tile(k, turn, first=False):
                hidden_out(k - 1)
                act.wait_ge(hidden_ready, k)
                silu(k)
                act.wait_ge(tail_copied, k)
                y_out(k - 1, (turn + 3) % 4, first)

            for key in STEPS:
                kind, misc = key[0], bank_of(key)
                if kind == "h_cols":
                    _, b, j = key
                    act.wait_ge(setup_dve, 4)
                    wait_filled(act, key)
                    act.activation(h_cols[b % 2][:, j, :], misc[:, :], ACT.Identity,
                                   bias=mod_cols[:, j, b:b + 1], scale=mod_cols[:, 2 + j, b:b + 1]).then_inc(act_evac, 1)
                elif kind == "values":
                    _, b, i = key
                    act.wait_ge(pool_const, V1_MADE if b else V0_MADE)
                    wait_filled(act, key)
                    act.activation(v_rows[b % 2][:, i, :, 0:HD], misc[:, 0:D].rearrange("p (h d) -> p h d", h=NH),
                                   ACT.Copy).then_inc(act_evac, 1)
                elif kind == "project":
                    _, u, w = key
                    wait_filled(act, key)
                    if u >= 1:
                        act.wait_ge(parts_stored[w], 16 * u)
                    act.activation(parts[w][:, 0, :], misc[:, :], ACT.Copy,
                                   scale=(HD ** -0.5, 1.0)[w]).then_inc(high_ready, 1)
                elif kind == "split":
                    _, u, w = key
                    wait_evacuated(act, ("project", u, w))
                    act.activation(parts[w][:, 1, :], rest[w], ACT.Copy).then_inc(mid_ready, 1)
                elif kind == "max_rows":
                    u = key[1]
                    wait_filled(act, key)
                    if u >= 1:
                        act.wait_ge(max_stored, 16 * u)
                    act.activation(max_parts[:, 0, :], misc[0:HU, :], ACT.Copy, scale=-1.0).then_inc(mhigh_ready, 1)
                elif kind == "max_split":
                    u = key[1]
                    wait_evacuated(act, ("max_rows", u))
                    act.activation(max_parts[:, 1, :], max_rest[:, :], ACT.Copy).then_inc(mmid_ready, 1)
                elif kind == "score":
                    _, g, n = key
                    k, h0, nh = score_slot(n)
                    w = T - k * P
                    s = SLOTS * g + n
                    if s == 0:
                        act.wait_ge(mod_stored, 16)
                    if g >= 1:
                        act.wait_ge(pv_done, 4 * (g - 1) + k + 1)
                    act.wait_ge(st_filled, s + 1)
                    src = st[s % ST][:, 0:nh * w].rearrange("p (h t) -> p h t", h=nh)
                    act.activation(probs[k][:, h0:h0 + nh, :], src, ACT.Exp).then_inc(exp_done, 1)
                elif kind == "value_sum":
                    _, g, k = key
                    if k == TT - 1:
                        act.wait_ge(pv_done, 4 * (g + 1))
                        if g >= 8:
                            wait_filled(act, ("z_rows", (g // 4 - 1) * TT - 1))
                        act.activation(z_cols[g // 4 % 2][:, g % 4, :], pv[:, :], ACT.Copy).then_inc(z_copied, 1)
                elif kind == "z_cols":
                    wait_filled(act, key)
                    act.activation(zn_cols[:, :, :].rearrange("p j t -> p (j t)"), misc[:, 0:D], ACT.Copy).then_inc(act_evac, 1)
                elif kind == "h2_cols":
                    t = key[1]
                    wait_filled(act, key)
                    act.activation(h2_cols[:, :, :].rearrange("p j t -> p (j t)"), misc[:, 0:D], ACT.Copy).then_inc(act_evac, 1)
                    act.activation(h2x[:, t % TT, 1, 0:D], h2x[:, t % TT, 0, 0:D], ACT.Copy).then_inc(h2_copied, 1)
                elif kind == "router":
                    t = key[1]
                    wait_filled(act, key)
                    if t >= TT:
                        act.wait_ge(shifted, t // TT)
                    act.activation(logits[:, t % TT, :], misc[:, 0:E], ACT.Copy).then_inc(act_evac, 1)
                elif kind == "tile":
                    k = key[1]
                    if k == 0:
                        silu(0)
                    else:
                        tile(k, k % 4, first=(k == 1))
                elif kind == "gate":
                    b = key[1]
                    act.wait_ge(shifted, b + 1)
                    act.activation(gate_exp[:, :, :], gate_t[:, :, :], ACT.Exp).then_inc(gate_exped, 1)

            with act.Fori(PEELED, TILES - 1, 4) as k:
                for n in range(4):
                    tile(k + n, (PEELED + n) % 4)
            tile(TILES - 1, (TILES - 1) % 4)
            hidden_out(TILES - 1)
            act.wait_ge(tail_copied, TILES)
            y_out(TILES - 1, (TILES - 1) % 4)

        @block.tensor
        def _(pe):
            pe.wait_ge(small_loaded, 16)
            pe.wait_ge(pool_const, IDENT_MADE)
            for j in range(DK):
                ins = pe.transpose(misc2[0][:, j * B:(j + 1) * B], c_sb[:, j * P:(j + 1) * P], ident[0:B, 0:B])
            ins.then_inc(setup_mm, 1)
            pe.wait_ge(c_ready, 1)

            def modulation(n):
                bank = (mx[0], mx[1], pv)[n][0:B, :]
                pe.wait_ge(wmod_loaded[n], 16)
                for j in range(DK):
                    ins = pe.matmul(bank, c_silu[:, j, :], wmod_sb[:, j, n * 512:(n + 1) * 512],
                                    start=(j == 0), stop=(j == DK - 1))
                ins.then_inc(setup_mm, 1)

            modulation(0)
            pe.wait_ge(setup_dve, 3)
            for m in range(4):
                ins = pe.transpose(misc2[0][:, m * B:(m + 1) * B], mod_rows[:, m * P:(m + 1) * P], ident[0:B, 0:B])
            ins.then_inc(setup_mm, 1)
            pe.wait_ge(setup_dve, 4)
            pe.wait_ge(attn_w_loaded, 80)

            def expert_of(k):
                return pe.value_load(table[0:1, 0, bass.ds(k, 1)], min_val=0, max_val=E - 1)

            def turn_rows(k):
                pe.wait_ge(xg_loaded, 16 * (k + 1))
                for j in range(DK):
                    ins = pe.transpose(st[1][:, j * P:(j + 1) * P], xg[:, j * P:(j + 1) * P], ident[:, :])
                ins.then_inc(xg_turned, 1)

            def up(k, e, col, bank, done):
                for j in range(DK):
                    w = arena[:, bass.ds(e * WCOLS + (col + j * F), F)]
                    ins = pe.matmul(bank[:, :], xg_cols[:, j, :], w, start=(j == 0), stop=(j == DK - 1))
                ins.then_inc(done, 1)

            def turn_hidden(k):
                pe.wait_ge(hidden_ready, k + 1)
                for j in range(FK):
                    ins = pe.transpose(pv[:, j * P:(j + 1) * P], hidden[:, j * P:(j + 1) * P], ident[:, :])
                ins.then_inc(hidden_turned, 1)

            def down(k, e, first=False):
                pe.wait_ge(hidden_copied, k + 1)
                if not first:
                    pe.wait_ge(y_copied, k)
                for j in range(FK):
                    w = arena[:, bass.ds(e * WCOLS + (W2 + j * D), D)]
                    ins = pe.matmul(st[0][:, 0:D], hidden_cols[:, j, :], w, start=(j == 0), stop=(j == FK - 1))
                ins.then_inc(y_mm, 1)

            def tile(k):
                e, e_before = expert_of(k), expert_of(k - 1)
                pe.wait_ge(cols_copied, k + 1)
                up(k, e, W1, mx[0], gate_mm)
                turn_hidden(k - 1)
                return e, e_before

            def middle(k, first=False):
                e, e_before = tile(k)
                turn_rows(k + 1)
                up(k, e, W3, mx[1], up_mm)
                down(k - 1, e_before, first)

            def tile_0():
                pe.wait_ge(first_w_loaded, 16 * 3 * EARLY)
                pe.wait_ge(last_w_loaded, 16 * 3 * (E - EARLY))
                pe.wait_ge(table_ready, 1)
                pe.wait_ge(exp_done, SLOTS * GROUPS)
                pe.wait_ge(z_copied, GROUPS)
                pe.wait_ge(mx_drained, FILLS * UNITS)
                turn_rows(0)
                pe.wait_ge(cols_copied, 1)
                e0 = expert_of(0)
                up(0, e0, W1, mx[0], gate_mm)
                turn_rows(1)
                up(0, e0, W3, mx[1], up_mm)

            for key in STEPS:
                kind = key[0]
                misc = bank_of(key)
                if key in use and use[key][0] >= 2:
                    wait_evacuated(pe, use_order[use[key][0] - 2])
                if kind == "h_cols":
                    _, b, j = key
                    pe.wait_ge(xn_ready, TT * (b + 1))
                    for i in range(TT):
                        ins = pe.transpose(misc[:, i * P:(i + 1) * P], xn[:, i, j * P:(j + 1) * P], ident[:, :])
                    ins.then_inc(misc_filled, 1)
                elif kind == "values":
                    _, b, i = key
                    wait_evacuated(pe, ("h_cols", b, 1))
                    for j in range(DK):
                        ins = pe.matmul(misc[:, 0:D], h_cols[b % 2][:, j, i * P:(i + 1) * P], wv_sb[:, j, :],
                                        start=(j == 0), stop=(j == DK - 1))
                    ins.then_inc(misc_filled, 1)
                elif kind == "project":
                    _, u, w = key
                    b, half = u // 2, u % 2
                    wait_evacuated(pe, ("h_cols", b, 1))
                    for j in range(DK):
                        ins = pe.matmul(misc[:, :], wqk_sb[:, w, j, half * P:(half + 1) * P], h_cols[b % 2][:, j, :],
                                        start=(j == 0), stop=(j == DK - 1))
                    ins.then_inc(misc_filled, 1)
                elif kind == "modulation":
                    modulation(1)
                    modulation(2)
                elif kind == "max_fill":
                    _, u, n = key
                    i, h0, nh = max_fill(n)
                    w = (i + 1) * P
                    f = FILLS * u + n
                    if n == 0 and u == 0:
                        pe.wait_ge(pool_const, CAUSAL_MADE)
                        pe.wait_ge(mod_ready, 1)
                    if n == 0:
                        pe.wait_ge(stack_loaded[u % STACKS], 16 * 2 * NTERMS * stack_turn(u))
                    if f >= 2:
                        pe.wait_ge(mx_drained, f - 1)
                    bank = mx[f % 2]
                    qs, ks = q_stack[u % STACKS], k_stack[u % STACKS]
                    for a in range(nh):
                        pe.matmul(bank[:, a * w:(a + 1) * w], qs[0:KS, h0 + a, i * P:(i + 1) * P], ks[0:KS, h0 + a, 0:w],
                                  start=(a == 0), stop=False, skip_group_check=True)
                    diag = bank[:, 0:nh * w].rearrange("p (h s) -> p h s", h=nh)[:, :, i * P:(i + 1) * P]
                    pe.matmul(diag, identb[:, :], causal[:, :].unsqueeze(1).to_broadcast([P, nh, P]),
                              start=False, stop=True, skip_group_check=True).then_inc(mx_filled, 1)
                elif kind == "max_rows":
                    u = key[1]
                    pe.wait_ge(mx_drained, FILLS * (u + 1))
                    for i in range(TT):
                        ins = pe.transpose(misc[0:HU, i * P:(i + 1) * P], row_max[:, u % 2, i, :], ident[:, :])
                    ins.then_inc(misc_filled, 1)
                elif kind == "score":
                    _, g, n = key
                    u = g // 2
                    k, h0, nh = score_slot(n)
                    w = T - k * P
                    s = SLOTS * g + n
                    if s >= ST:
                        pe.wait_ge(exp_done, s - ST + 1)
                    if s == 0:
                        pe.wait_ge(ones_made, STACKS)
                    if n == 0 and g % 2 == 0:
                        pe.wait_ge(max_loaded[u % STACKS], 16 * stack_turn(u))
                    qs, ks = q_stack[u % STACKS], k_stack[u % STACKS]
                    for a in range(nh):
                        h = (g % 2) * HG + h0 + a
                        pe.matmul(st[s % ST][:, a * w:(a + 1) * w], ks[0:KB, h, k * P:(k + 1) * P],
                                  qs[0:KB, h, k * P:T], start=(a == 0), stop=False, skip_group_check=True)
                    diag = st[s % ST][:, 0:nh * w].rearrange("p (h t) -> p h t", h=nh)[:, :, 0:P]
                    pe.matmul(diag, causal[:, :], identb[:, :].unsqueeze(1).to_broadcast([P, nh, P]),
                              start=False, stop=True, skip_group_check=True).then_inc(st_filled, 1)
                elif kind == "value_sum":
                    _, g, k = key
                    b = g // 4
                    pe.wait_ge(exp_done, SLOTS * g + LAST_SLOT[k] + 1)
                    if k == 0:
                        wait_evacuated(pe, ("values", b, TT - 1))
                        if g >= 1:
                            pe.wait_ge(z_copied, g)
                    for a in range(HG):
                        h = (g % 4) * HG + a
                        ins = pe.matmul(pv[32 * a:32 * a + 32, k * P:T], v_rows[b % 2][:, k, h, :], probs[k][:, a, :],
                                        start=(k == 0), stop=(k == TT - 1), skip_group_check=True)
                    ins.then_inc(pv_done, 1)
                elif kind == "z_rows":
                    t = key[1]
                    b, i = t // TT, t % TT
                    pe.wait_ge(z_copied, 4 * (b + 1))
                    for g in range(4):
                        ins = pe.transpose(misc[:, g * P:(g + 1) * P], z_cols[b % 2][:, g, i * P:(i + 1) * P], ident[:, :])
                    ins.then_inc(misc_filled, 1)
                elif kind == "z_cols":
                    t = key[1]
                    wait_evacuated(pe, ("z_rows", t))
                    for j in range(DK):
                        ins = pe.transpose(misc[:, j * P:(j + 1) * P],
                                           zn[:, j * HU:(j + 1) * HU, :].rearrange("p h d -> p (h d)"), ident[:, :])
                    ins.then_inc(misc_filled, 1)
                elif kind == "out_rows":
                    t = key[1]
                    wait_evacuated(pe, ("z_cols", t))
                    pe.wait_ge(wog_ready, t // TT + 1)
                    for j in range(DK):
                        ins = pe.matmul(misc[:, 0:D], zn_cols[:, j, :], wog[:, j, :], start=(j == 0), stop=(j == DK - 1))
                    ins.then_inc(misc_filled, 1)
                elif kind == "h2_cols":
                    t = key[1]
                    pe.wait_ge(h2_ready, t + 1)
                    for j in range(DK):
                        ins = pe.transpose(misc[:, j * P:(j + 1) * P], h2x[:, t % TT, 0, j * P:(j + 1) * P], ident[:, :])
                    ins.then_inc(misc_filled, 1)
                elif kind == "router":
                    t = key[1]
                    wait_evacuated(pe, ("h2_cols", t))
                    for j in range(DK):
                        ins = pe.matmul(misc[:, 0:E], h2_cols[:, j, :], gate_sb[:, j, :], start=(j == 0), stop=(j == DK - 1))
                    ins.then_inc(misc_filled, 1)
                elif kind == "tile":
                    if key[1] == 0:
                        tile_0()
                    else:
                        middle(key[1], first=(key[1] == 1))
                elif kind == "counts":
                    b = (B - 2, B - 1)[key[1]]
                    pe.wait_ge(chosen_ready, b + 1)
                    pe.matmul(misc[:, 0:E], onesb[:, :], before[:, (b + 1) * TT, :], start=True, stop=True).then_inc(misc_filled, 1)
                elif kind == "rank":
                    b = key[1]
                    pe.wait_ge(chosen_ready, b + 1)
                    if b == 0:
                        pe.wait_ge(pool_const, CONSTS)
                    for i in range(TT):
                        t = b * TT + i
                        pe.matmul(misc[:, i * E:(i + 1) * E], earlier[:, :], chosen[:, t, :],
                                  start=(i == 0), stop=False, skip_group_check=True)
                        ins = pe.matmul(misc[:, i * E:(i + 1) * E], onesb[:, :], before[:, t, :],
                                        start=False, stop=(i == TT - 1), skip_group_check=True)
                    ins.then_inc(misc_filled, 1)
            with pe.Fori(PEELED, TILES - 1) as k:
                middle(k)
            e, e_before = tile(TILES - 1)
            up(TILES - 1, e, W3, mx[1], up_mm)
            down(TILES - 2, e_before)
            turn_hidden(TILES - 1)
            down(TILES - 1, e)

        @block.vector
        def _(dve):
            steps = [0]

            def own(ins):
                steps[0] += 1
                ins.then_inc(vec_step, 1)
                dve.wait_ge(vec_step, steps[0])

            dve.wait_ge(setup_mm, 1)
            dve.tensor_copy(c_cols[:, :, :].rearrange("p j b -> p (j b)"), misc2[0][:, 0:DK * B]).then_inc(setup_dve, 1)
            dve.wait_ge(c_step, 1)
            own(dve.tensor_scalar(c_exp[:, :, :], c_exp[:, :, :], 1.0, None, ALU.add))
            own(dve.reciprocal(c_silu[:, :, :], c_exp[:, :, :]))
            dve.tensor_tensor(c_silu[:, :, :], c_silu[:, :, :], c_cols[:, :, :], ALU.mult).then_inc(c_ready, 1)

            def modulation_columns():
                dve.wait_ge(setup_mm, 2)
                dve.tensor_copy(mod_rows[:, 0:D], mx[0][0:B, 0:D]).then_inc(setup_dve, 1)
                dve.tensor_scalar(mod_rows[:, D:2 * D], mx[0][0:B, D:2 * D], 1.0, None, ALU.add).then_inc(setup_dve, 1)
                dve.wait_ge(setup_mm, 3)
                dve.tensor_copy(mod_cols[:, :, :].rearrange("p n b -> p (n b)"), misc2[0][:, 0:4 * B]).then_inc(setup_dve, 1)

            def modulation_rows():
                dve.wait_ge(setup_mm, 5)
                own(dve.tensor_scalar(mod_rows[:, 4 * D:5 * D], pv[0:B, 0:D], 1.0, None, ALU.add))
                own(dve.tensor_copy(mod_rows[:, 3 * D:4 * D], mx[1][0:B, D:2 * D]))
                for n, src in enumerate((mx[1][0:B, 0:D], pv[0:B, D:2 * D])):
                    own(dve.tensor_scalar(gtmp[:, 0, :], src, 0.0, 2.0, ALU.is_ge, ALU.mult))
                    own(dve.tensor_scalar(gtmp[:, 0, :], gtmp[:, 0, :], -1.0, None, ALU.add))
                    own(dve.tensor_scalar(gtmp[:, 1, :], src, -1.0, None, ALU.mult))
                    own(dve.tensor_tensor(gtmp[:, 1, :], gtmp[:, 1, :], src, ALU.max))
                    own(dve.tensor_scalar(gtmp[:, 1, :], gtmp[:, 1, :], 0.25, None, ALU.max))
                    ins = dve.tensor_tensor(mod_rows[:, (2 + 3 * n) * D:(3 + 3 * n) * D], gtmp[:, 0, :], gtmp[:, 1, :], ALU.mult)
                    if n == 0:
                        own(ins)
                ins.then_inc(mod_ready, 1)

            def count_tiles(stage, misc):
                if stage == 0:
                    dve.tensor_copy(count_f[:, :], misc[0:1, 0:E]).then_inc(dve_evac, 1)
                else:
                    own(dve.tensor_tensor(fill_f[:, :], misc[:, 0:E], part_base[:, :], ALU.add))
                    dve.tensor_scalar(count_f[:, :], misc[0:1, 0:E], float(P - 1), None, ALU.add).then_inc(dve_evac, 1)
                    dve.tensor_copy(fill_i[:, :], fill_f[:, :]).then_inc(fill_ready, 1)
                wait_evacuated(dve, ("counts", stage))
                own(dve.tensor_copy(count_i[:, :], count_f[:, :]))
                own(dve.tensor_single_scalar(count_i[:, :], count_i[:, :], 7, ALU.logical_shift_right))
                own(dve.tensor_copy(ntile[:, :], count_i[:, :]))
                if stage == 1:
                    own(dve.tensor_tensor(ntile[:, :], ntile[:, :], took[:, :], ALU.subtract))
                own(dve.tensor_copy(ends[:, 0, :], ntile[:, :]))
                for n, d in enumerate((1, 2, 4)):
                    own(dve.tensor_copy(ends[:, n + 1, 0:d], ends[:, n, 0:d]))
                    own(dve.tensor_tensor(ends[:, n + 1, d:E], ends[:, n, d:E], ends[:, n, 0:E - d], ALU.add))

            def fill_table(stage):
                n, to = ((FIRST, 0), (TILES - FIRST, FIRST))[stage]
                end = ends[:, 3, :]
                wide = [1, n, E]
                if stage == 1:
                    own(dve.tensor_tensor(ntile[:, :], ntile[:, :], took[:, :], ALU.add))
                    own(dve.tensor_tensor(ntile[:, 0:E - 1], ntile[:, 0:E - 1], took[:, 1:E], ALU.subtract))
                a, b = tab_a[:, 0:n, :], tab_b[:, 0:n, :]
                own(dve.tensor_tensor(a, tile_no[:, 0:n].unsqueeze(2).to_broadcast(wide),
                                      end.unsqueeze(1).to_broadcast(wide), ALU.is_ge))
                own(dve.tensor_tensor(b, a, ntile[:, :].unsqueeze(1).to_broadcast(wide), ALU.mult))
                own(dve.tensor_reduce(tab_v[:, 0, 0:n], a, AX_X, ALU.add))
                own(dve.tensor_reduce(tab_v[:, 1, 0:n], b, AX_X, ALU.add))
                own(dve.tensor_tensor(tab_v[:, 2, 0:n], tile_no[:, 0:n], tab_v[:, 1, 0:n], ALU.subtract))
                if stage == 1:
                    own(dve.tensor_scalar(tab_v[:, 2, 0:n], tab_v[:, 2, 0:n], took[:, 0:1], None, ALU.add))
                own(dve.tensor_scalar(tab_v[:, 2, 0:n], tab_v[:, 2, 0:n], float(P), None, ALU.mult))
                own(dve.scalar_tensor_tensor(out=tab_v[:, 3, 0:n], in0=tab_v[:, 0, 0:n], scalar=float(REGION),
                                             in1=tab_v[:, 2, 0:n], op0=ALU.mult, op1=ALU.add))
                if stage == 0:
                    own(dve.tensor_tensor(took[:, :], end, ntile[:, :], ALU.subtract))
                    own(dve.tensor_scalar(took[:, :], took[:, :], -1.0, float(FIRST), ALU.mult, ALU.add))
                    own(dve.tensor_scalar(took[:, :], took[:, :], 0.0, None, ALU.max))
                    own(dve.tensor_tensor(took[:, :], took[:, :], ntile[:, :], ALU.min))
                else:
                    own(dve.tensor_scalar(tab_v[:, 3, 0:n], tab_v[:, 3, 0:n], float(NULL_ROW), None, ALU.min))
                    own(dve.tensor_scalar(tab_v[:, 0, 0:n], tab_v[:, 0, 0:n], float(E - 1), None, ALU.min))
                own(dve.tensor_copy(table[:, 0, to:to + n], tab_v[:, 0, 0:n]))
                dve.tensor_copy(table[:, 1, to:to + n], tab_v[:, 3, 0:n]).then_inc(table_ready, 1)

            def rows_out(k, turn, first=False):
                dve.wait_ge(xg_turned, k + 1)
                dve.tensor_copy(xg_cols.rearrange("p j t -> p (j t)"), st[1][:, 0:D]).then_inc(cols_copied, 1)
                if not first:
                    dve.wait_ge(y_stored, 16 * (k - 3))
                dve.tensor_copy(tail[turn].bitcast(I32), xg[:, DEST:DEST + 2].bitcast(I32)).then_inc(tail_copied, 1)

            def gated(k):
                dve.wait_ge(silu_done, k + 1)
                dve.wait_ge(up_mm, k + 1)
                dve.tensor_tensor(hidden, silu_sb, mx[1][:, :], ALU.mult).then_inc(hidden_ready, 1)

            def tile(k, turn, first=False):
                gated(k)
                rows_out(k + 1, (turn + 1) % 4, first)

            for key in STEPS:
                kind, misc = key[0], bank_of(key)
                if kind == "tile":
                    k = key[1]
                    if k == 0:
                        rows_out(0, 0, first=True)
                    tile(k, k % 4, first=(k < 3))
                elif kind == "counts":
                    wait_filled(dve, key)
                    count_tiles(key[1], misc)
                elif kind == "table":
                    fill_table(key[1])
                elif kind == "norm_stats":
                    b = key[1]
                    dve.wait_ge(x_loaded[b], 16)
                    if b >= 1:
                        dve.wait_ge(rstd_ready, b)
                    for i in range(TT):
                        own(dve.bn_stats(stats[:, i, :], xs[:, b * TT + i, :]))
                        ins = dve.bn_aggr(moments[:, i, :], stats[:, i, :])
                        if i < TT - 1:
                            own(ins)
                    ins.then_inc(stats_ready, 1)
                elif kind == "norm_rows":
                    b = key[1]
                    dve.wait_ge(rstd_ready, b + 1)
                    if b >= 1:
                        wait_filled(dve, ("h_cols", b - 1, 1))
                    for i in range(TT):
                        dve.tensor_scalar(xn[:, i, :], xs[:, b * TT + i, :], moments[:, i, 0:1], rstd[:, i:i + 1],
                                          ALU.subtract, ALU.mult).then_inc(xn_ready, 1)
                    if b == 0:
                        modulation_columns()
                elif kind == "modulation":
                    modulation_rows()
                elif kind == "ones":
                    dve.memset(k_stack[key[1]][96:128, :, :].bitcast(F32), TWO_ONES).then_inc(ones_made, 1)
                elif kind == "project":
                    _, u, w = key
                    n = 2 * u + w
                    dve.wait_ge(high_ready, n + 1)
                    if n >= 2:
                        dve.wait_ge(low_ready, n - 1)
                    dve.scalar_tensor_tensor(out=rest[w], in0=misc[:, :], scalar=(HD ** -0.5, 1.0)[w],
                                             in1=parts[w][:, 0, :], op0=ALU.mult, op1=ALU.subtract).then_inc(dve_evac, 1)
                elif kind == "max_fill":
                    _, u, n = key
                    i, h0, nh = max_fill(n)
                    w = (i + 1) * P
                    f = FILLS * u + n
                    if n == 0 and u >= 2:
                        wait_filled(dve, ("max_rows", u - 2))
                    dve.wait_ge(mx_filled, f + 1)
                    dve.tensor_reduce(row_max[:, u % 2, i, h0:h0 + nh],
                                      mx[f % 2][:, 0:nh * w].rearrange("p (h s) -> p h s", h=nh), AX_X, ALU.max).then_inc(mx_drained, 1)
                elif kind == "max_rows":
                    u = key[1]
                    dve.wait_ge(mhigh_ready, u + 1)
                    if u >= 1:
                        dve.wait_ge(mlow_ready, u)
                    dve.scalar_tensor_tensor(out=max_rest[:, :], in0=misc[0:HU, :], scalar=-1.0,
                                             in1=max_parts[:, 0, :], op0=ALU.mult, op1=ALU.subtract).then_inc(dve_evac, 1)
                elif kind == "z_rows":
                    t = key[1]
                    wait_filled(dve, key)
                    z = misc[:, :].rearrange("p (h d) -> p h d", h=NH)
                    own(dve.reciprocal(z_recip[:, :], z[:, :, HD]))
                    dve.tensor_tensor(zn[:, :, :], z[:, :, 0:HD], z_recip[:, :].unsqueeze(2).to_broadcast([P, NH, HD]),
                                      ALU.mult).then_inc(dve_evac, 1)
                elif kind == "out_rows":
                    t = key[1]
                    wait_filled(dve, key)
                    dve.tensor_tensor(xs[:, t, :], misc[:, 0:D], xs[:, t, :], ALU.add).then_inc(dve_evac, 1)
                    wait_evacuated(dve, key)
                    if t >= 2:
                        dve.wait_ge(rstd2_ready, t - 1)
                    own(dve.bn_stats(stats2[:, :], xs[:, t, :]))
                    dve.bn_aggr(moments2[:, t % 2, :], stats2[:, :]).then_inc(stats2_ready, 1)
                elif kind == "norm2":
                    t = key[1]
                    b, i = t // TT, t % TT
                    dve.wait_ge(rstd2_ready, t + 1)
                    if b >= 1:
                        dve.wait_ge(scattered[i], 16 * 2 * b)
                    dve.tensor_scalar(h2x[:, i, 0, 0:D], xs[:, t, :], moments2[:, t % 2, 0:1], rstd2[:, t % 2:t % 2 + 1],
                                      ALU.subtract, ALU.mult).then_inc(xn2_ready, 1)
                elif kind == "gate":
                    b = key[1]
                    wait_evacuated(dve, ("router", b * TT + TT - 1))
                    own(dve.tensor_reduce(gate_s[:, 0, :], logits[:, :, :], AX_X, ALU.max))
                    dve.tensor_tensor(gate_t[:, :, :], logits[:, :, :], gate_s[:, 0, :].unsqueeze(2).to_broadcast([P, TT, E]),
                                      ALU.subtract).then_inc(shifted, 1)
                elif kind == "choose":
                    _, b, part = key
                    wide = [P, TT, E]
                    rev = rev_e[:, :].unsqueeze(1).to_broadcast(wide)
                    if part == 0:
                        dve.wait_ge(gate_exped, b + 1)
                        if b == 0:
                            dve.wait_ge(pool_const, CONSTS)
                        own(dve.tensor_reduce(gate_s[:, 1, :], gate_exp[:, :, :], AX_X, ALU.add))
                        own(dve.reciprocal(gate_s[:, 2, :], gate_s[:, 1, :]))
                        own(dve.tensor_tensor(gate_p[:, :, :], gate_exp[:, :, :], gate_s[:, 2, :].unsqueeze(2).to_broadcast(wide), ALU.mult))
                    elif part < 3:
                        n = part - 1
                        own(dve.tensor_reduce(top_w[:, n, :], gate_p[:, :, :], AX_X, ALU.max))
                        own(dve.tensor_tensor(gate_t[:, :, :], gate_p[:, :, :], top_w[:, n, :].unsqueeze(2).to_broadcast(wide), ALU.is_equal))
                        own(dve.tensor_tensor(gate_t[:, :, :], gate_t[:, :, :], rev, ALU.mult))
                        own(dve.tensor_reduce(gate_s[:, 3, :], gate_t[:, :, :], AX_X, ALU.max))
                        own(dve.tensor_tensor(hot[:, n], rev, gate_s[:, 3, :].unsqueeze(2).to_broadcast(wide), ALU.is_equal))
                        if n == 0:
                            own(dve.scalar_tensor_tensor(out=gate_p[:, :, :], in0=hot[:, 0], scalar=-2.0, in1=gate_p[:, :, :],
                                                         op0=ALU.mult, op1=ALU.add))
                    else:
                        own(dve.tensor_tensor(chosen[:, b * TT:(b + 1) * TT, :], hot[:, 0], hot[:, 1], ALU.add))
                        for i in range(TT):
                            t = b * TT + i
                            ins = dve.tensor_tensor(before[:, t + 1, :], before[:, t, :], chosen[:, t, :], ALU.add)
                            if i < TT - 1:
                                own(ins)
                        ins.then_inc(chosen_ready, 1)
                elif kind == "rank":
                    b = key[1]
                    wide = [P, TT, E]
                    wait_filled(dve, key)
                    dve.tensor_tensor(rank_pos[:, :, :], misc[:, 0:TT * E].rearrange("p (i e) -> p i e", i=TT),
                                      base_e[:, :].unsqueeze(1).to_broadcast(wide), ALU.add).then_inc(dve_evac, 1)
                    wait_evacuated(dve, key)
                    for n in range(2):
                        own(dve.tensor_tensor(gate_t[:, :, :], rank_pos[:, :, :], hot[:, n], ALU.mult))
                        own(dve.tensor_reduce(pos_f[:, n, :], gate_t[:, :, :], AX_X, ALU.add))
                        own(dve.tensor_copy(h2x[:, :, n, DEST].bitcast(I32), dest[:, n, b * TT:(b + 1) * TT]))
                        own(dve.tensor_copy(h2x[:, :, n, WEIGHT], top_w[:, n, :]))
                    dve.tensor_copy(pos_i[:, :, :], pos_f[:, :, :]).then_inc(routed, 1)
            with dve.Fori(PEELED, TILES - 1, 4) as k:
                for n in range(4):
                    tile(k + n, (PEELED + n) % 4)
            gated(TILES - 1)

            for n in range(PIECES + 2):
                if n < PIECES:
                    tiles = slice(n * PIECE, (n + 1) * PIECE)
                    if n % 2 == 0:
                        dve.wait_ge(y_loaded[n], 32)
                        dve.tensor_tensor(ya[:, tiles, :], ya[:, tiles, :], yb[:, tiles, :], ALU.add).then_inc(y_summed[0], 1)
                if 1 <= n <= PIECES:
                    tiles = slice((n - 1) * PIECE, n * PIECE)
                    gb = mods[:, (n - 1) * PIECE // TT, 3, :]
                    dve.wait_ge(y_summed[(n - 1) % 2], (n - 1) // 2 + 1)
                    dve.tensor_tensor(ya[:, tiles, :], ya[:, tiles, :], gb.unsqueeze(1).to_broadcast([P, PIECE, D]),
                                      ALU.mult).then_inc(y_gated, 1)
                if n >= 2:
                    tiles = slice((n - 2) * PIECE, (n - 1) * PIECE)
                    dve.wait_ge(y_gated, n - 1)
                    dve.tensor_tensor(xs[:, tiles, :], xs[:, tiles, :], ya[:, tiles, :], ALU.add).then_inc(out_ready, 1)


def kernel(**inputs):
    import numpy as np
    import concourse.bacc as bacc
    from concourse.bass_utils import run_bass_kernel_spmd

    def laid(name, turn=False):
        a = np.asarray(inputs[name])
        return np.ascontiguousarray(a.T if turn else a)

    arrays = {
        "x": laid("L0_attn_x"),
        "wq": laid("L0_attn_Wq", True),
        "wk": laid("L0_attn_Wk", True),
        "wv": laid("L0_attn_Wv", True),
        "wo": laid("L0_attn_Wo", True),
        "gate_w": laid("L0_ffn_gate_w"),
        "w1": laid("L0_ffn_w1"),
        "w3": laid("L0_ffn_w3"),
        "w2": laid("L0_ffn_w2"),
        "c": laid("L0_c"),
        "wmod": laid("L0_wmod"),
    }
    nc = bacc.Bacc("TRN2", target_bir_lowering=False, num_devices=1)
    aps = [nc.dram_tensor(n, a.shape, mybir.dt.from_np(a.dtype), kind="ExternalInput").ap() for n, a in arrays.items()]
    out = nc.dram_tensor("out", [B, T, D], F32, kind="ExternalOutput").ap()
    build(nc, *aps, out)
    r = run_bass_kernel_spmd(nc, [arrays], core_ids=[0])
    return r.results[0]["out"]
```
